# Optimizing a Trainium2 kernel written in Bass

```python
import numpy as np
import jax
import jax.numpy as jnp

def _softmax(x, axis=-1):
    return jax.nn.softmax(x, axis=axis)
def _gelu(x):
    return jax.nn.gelu(x, approximate=True)
def _silu(x):
    return jax.nn.silu(x)
def _sigmoid(x):
    return jax.nn.sigmoid(x)
def _layernorm(x, axis=-1, eps=1e-5):
    m = jnp.mean(x, axis=axis, keepdims=True)
    v = jnp.var(x, axis=axis, keepdims=True)
    return (x - m) / jnp.sqrt(v + eps)
def _scatter_add(tgt, idx, src, axis=0):
    return tgt.at[idx].add(src)
def _segment_sum(src, seg, n):
    return jax.ops.segment_sum(src, seg, n)

kernel_name = 'mk_metaformer_d1_conv_nchw512_c7bd1d'

def setup_inputs(seed: int = 0):
    np.random.seed(seed)
    _w = jnp.asarray
    def _rec_inputs():
        import jax
        import jax.numpy as jnp
        _gk = jax.random.key(seed)
        x = -0.0002928 + 1 * jax.random.normal(jax.random.fold_in(_gk, 1), (8, 512, 32, 32), jnp.float32)
        return x
    x = _rec_inputs()
    def _L0_conv_setup():
        import jax, jax.numpy as jnp
        import numpy as np
        C = 512
        NUM_HEADS = 8
        HEAD_DIM = C // NUM_HEADS
        if __name__ == '__main__':
            o = reference(**setup_inputs())
            print(o.shape)
        key = jax.random.key(seed)
        ks = jax.random.split(key, 9)
        s = 1.0 / np.sqrt(C)
        x = jax.random.normal(ks[0], (8, C, 32, 32), dtype=jnp.float32)
        Wq = jax.random.uniform(ks[1], (C, C), jnp.float32, -s, s)
        bq = jax.random.uniform(ks[2], (C,), jnp.float32, -s, s)
        Wk = jax.random.uniform(ks[3], (C, C), jnp.float32, -s, s)
        bk = jax.random.uniform(ks[4], (C,), jnp.float32, -s, s)
        Wv = jax.random.uniform(ks[5], (C, C), jnp.float32, -s, s)
        bv = jax.random.uniform(ks[6], (C,), jnp.float32, -s, s)
        Wo = jax.random.uniform(ks[7], (C, C), jnp.float32, -s, s)
        bo = jax.random.uniform(ks[8], (C,), jnp.float32, -s, s)
        return {'x': x, 'Wq': Wq, 'bq': bq, 'Wk': Wk, 'bk': bk, 'Wv': Wv, 'bv': bv, 'Wo': Wo, 'bo': bo}
    _L0_conv_all = _L0_conv_setup()
    _L0_conv_in = {k: v for k, v in _L0_conv_all.items() if k in ('Wq', 'bq', 'Wk', 'bk', 'Wv', 'bv', 'Wo', 'bo', )}
    del _L0_conv_all

    def _L0_ffn_setup():
        import jax, jax.numpy as jnp
        import numpy as np
        MARK_AX, OP_ADD, OP_SUB = (0, 1, 2)
        ALU_LO, ALU_HI = (16, 32)
        AX_CARRY_LO, AX_CARRY_HI = (48, 64)
        OPCODE_BASE = 80
        OUTPUT_LO, OUTPUT_HI, CARRY = (128, 144, 160)
        NIB_A, NIB_B, OP_START = (0, 1, 10)
        RESULT, CARRY_OUT = (100, 101)
        GE_POS, GE_DIM = (8, 160)
        OPC_ADD, OPC_SUB = (25, 26)
        B, S, D = (8, 4096, 512)

        def _decode_nibble(x, base):
            return jnp.argmax(x[..., base:base + 16] > 0.5, axis=-1).astype(x.dtype)

        def _pipeline(h, W, b):
            for i in range(3):
                h = jnp.einsum('bspd,od->bspo', h, W[i]) + b[i]
                if i < 2:
                    h = jax.nn.relu(h)
            return h
        key = jax.random.key(seed)
        kx, k1, k2, k3, k4 = jax.random.split(key, 5)
        x_bd = jax.random.uniform(kx, (B, S, D), dtype=jnp.float32)
        Wa = jax.random.normal(k1, (3, GE_DIM, GE_DIM), dtype=jnp.float32) * 0.05
        ba = jax.random.normal(k2, (3, GE_DIM), dtype=jnp.float32) * 0.05
        Ws = jax.random.normal(k3, (3, GE_DIM, GE_DIM), dtype=jnp.float32) * 0.05
        bs = jax.random.normal(k4, (3, GE_DIM), dtype=jnp.float32) * 0.05
        return {'x_bd': x_bd, 'Wa': Wa, 'ba': ba, 'Ws': Ws, 'bs': bs}
    _L0_ffn_all = _L0_ffn_setup()
    _L0_ffn_in = {k: v for k, v in _L0_ffn_all.items() if k in ('Wa', 'ba', 'Ws', 'bs', )}
    del _L0_ffn_all

    return {
        "x": x,
        "L0_conv_Wq": _L0_conv_in["Wq"],
        "L0_conv_bq": _L0_conv_in["bq"],
        "L0_conv_Wk": _L0_conv_in["Wk"],
        "L0_conv_bk": _L0_conv_in["bk"],
        "L0_conv_Wv": _L0_conv_in["Wv"],
        "L0_conv_bv": _L0_conv_in["bv"],
        "L0_conv_Wo": _L0_conv_in["Wo"],
        "L0_conv_bo": _L0_conv_in["bo"],
        "L0_ffn_Wa": _L0_ffn_in["Wa"],
        "L0_ffn_ba": _L0_ffn_in["ba"],
        "L0_ffn_Ws": _L0_ffn_in["Ws"],
        "L0_ffn_bs": _L0_ffn_in["bs"],
    }

def reference(x, L0_conv_Wq, L0_conv_bq, L0_conv_Wk, L0_conv_bk, L0_conv_Wv, L0_conv_bv, L0_conv_Wo, L0_conv_bo, L0_ffn_Wa, L0_ffn_ba, L0_ffn_Ws, L0_ffn_bs):
    import jax
    import jax.numpy as jnp
    def _L0_conv_ref(x, Wq, bq, Wk, bk, Wv, bv, Wo, bo):
        import jax, jax.numpy as jnp
        import numpy as np
        C = 512
        NUM_HEADS = 8
        HEAD_DIM = C // NUM_HEADS
        if __name__ == '__main__':
            o = reference(**setup_inputs())
            print(o.shape)
        N, Cc, H, W = x.shape
        S = H * W
        xs = x.reshape(N, Cc, S).transpose(0, 2, 1)
        q = xs @ Wq.T + bq
        k = xs @ Wk.T + bk
        v = xs @ Wv.T + bv
        q = q.reshape(N, S, NUM_HEADS, HEAD_DIM).transpose(0, 2, 1, 3)
        k = k.reshape(N, S, NUM_HEADS, HEAD_DIM).transpose(0, 2, 1, 3)
        v = v.reshape(N, S, NUM_HEADS, HEAD_DIM).transpose(0, 2, 1, 3)
        energy = jnp.einsum('nhqd,nhkd->nhqk', q, k)
        attn = jax.nn.softmax(energy / np.sqrt(HEAD_DIM), axis=3)
        out = jnp.einsum('nhql,nhld->nhqd', attn, v)
        out = out.reshape(N, Cc, S) if False else out.reshape(N, -1, Cc)
        out = out @ Wo.T + bo
        return out.reshape(N, Cc, H, W)

    def _L0_ffn_ref(x_bd, Wa, ba, Ws, bs):
        import jax, jax.numpy as jnp
        import numpy as np
        MARK_AX, OP_ADD, OP_SUB = (0, 1, 2)
        ALU_LO, ALU_HI = (16, 32)
        AX_CARRY_LO, AX_CARRY_HI = (48, 64)
        OPCODE_BASE = 80
        OUTPUT_LO, OUTPUT_HI, CARRY = (128, 144, 160)
        NIB_A, NIB_B, OP_START = (0, 1, 10)
        RESULT, CARRY_OUT = (100, 101)
        GE_POS, GE_DIM = (8, 160)
        OPC_ADD, OPC_SUB = (25, 26)
        B, S, D = (8, 4096, 512)

        def _decode_nibble(x, base):
            return jnp.argmax(x[..., base:base + 16] > 0.5, axis=-1).astype(x.dtype)

        def _pipeline(h, W, b):
            for i in range(3):
                h = jnp.einsum('bspd,od->bspo', h, W[i]) + b[i]
                if i < 2:
                    h = jax.nn.relu(h)
            return h
        x = x_bd
        Bsz, seq, _ = x.shape
        x_ge = jnp.zeros((Bsz, seq, GE_POS, GE_DIM), dtype=x.dtype)
        x_ge = x_ge.at[..., 0, NIB_A].set(_decode_nibble(x, ALU_LO))
        x_ge = x_ge.at[..., 1, NIB_A].set(_decode_nibble(x, ALU_HI))
        x_ge = x_ge.at[..., 0, NIB_B].set(_decode_nibble(x, AX_CARRY_LO))
        x_ge = x_ge.at[..., 1, NIB_B].set(_decode_nibble(x, AX_CARRY_HI))
        x_ge = x_ge.at[..., :, OP_START + OPC_ADD].set(x[..., OPCODE_BASE + OPC_ADD][..., None])
        x_ge = x_ge.at[..., :, OP_START + OPC_SUB].set(x[..., OPCODE_BASE + OPC_SUB][..., None])
        mark = x[..., MARK_AX] > 0.5
        m_add = mark & (x[..., OP_ADD] > 0.5)
        m_sub = mark & ~(x[..., OP_ADD] > 0.5) & (x[..., OP_SUB] > 0.5)
        active = (m_add | m_sub).astype(x.dtype)
        y_add = _pipeline(x_ge, Wa, ba)
        y_sub = _pipeline(x_ge, Ws, bs)
        y = jnp.where(m_add[..., None, None], y_add, jnp.where(m_sub[..., None, None], y_sub, x_ge))
        res_lo = jnp.clip(jnp.round(y[..., 0, RESULT]), 0, 15).astype(jnp.int32)
        res_hi = jnp.clip(jnp.round(y[..., 1, RESULT]), 0, 15).astype(jnp.int32)
        oh_lo = jax.nn.one_hot(res_lo, 16, dtype=x.dtype) * active[..., None]
        oh_hi = jax.nn.one_hot(res_hi, 16, dtype=x.dtype) * active[..., None]
        carry = (jnp.round(y[..., 1, CARRY_OUT]) > 0.5).astype(x.dtype) * active
        out = x
        out = out.at[..., OUTPUT_LO:OUTPUT_LO + 16].add(2.0 * oh_lo)
        out = out.at[..., OUTPUT_HI:OUTPUT_HI + 16].add(2.0 * oh_hi)
        out = out.at[..., CARRY].add(carry)
        return out

    def _gn(v, G=32, eps=1e-5):
        B_, C_, H_, W_ = v.shape
        g = v.reshape(B_, G, C_ // G, H_, W_)
        m = jnp.mean(g, axis=(2, 3, 4), keepdims=True)
        s = jnp.var(g, axis=(2, 3, 4), keepdims=True)
        return ((g - m) / jnp.sqrt(s + eps)).reshape(v.shape)

    def _ln_c(v, eps=1e-6):
        m = jnp.mean(v, axis=1, keepdims=True)
        s = jnp.var(v, axis=1, keepdims=True)
        return (v - m) / jnp.sqrt(s + eps)

    def _ln_t(v, eps=1e-5):
        m = jnp.mean(v, axis=-1, keepdims=True)
        s = jnp.var(v, axis=-1, keepdims=True)
        return (v - m) / jnp.sqrt(s + eps)

    def _to_tokens(v):
        B_, C_, H_, W_ = v.shape
        return v.reshape(B_, C_, H_ * W_).transpose(0, 2, 1)
    def _from_tokens(t, like):
        B_, C_, H_, W_ = like.shape
        return t.transpose(0, 2, 1).reshape(B_, C_, H_, W_)

    x = x + _L0_conv_ref(_ln_c(x), L0_conv_Wq, L0_conv_bq, L0_conv_Wk, L0_conv_bk, L0_conv_Wv, L0_conv_bv, L0_conv_Wo, L0_conv_bo)
    t = _to_tokens(x)
    t = t + _L0_ffn_ref(_ln_t(t), L0_ffn_Wa, L0_ffn_ba, L0_ffn_Ws, L0_ffn_bs)
    x = _from_tokens(t, x)
    return x


_drawn_inputs = setup_inputs


def setup_inputs(seed=0):
    import zlib

    import numpy as np

    out = dict(_drawn_inputs(seed))
    spreads = {}
    factors = {'L0_conv_Wq': 8.0,
     'L0_conv_bq': 8.0,
     'L0_conv_Wk': 8.0,
     'L0_conv_bk': 64.0,
     'L0_conv_Wv': 4.654,
     'L0_conv_bv': 3.855,
     'L0_conv_Wo': 2.982,
     'L0_conv_bo': 12.14}
    for name, (base, spread) in spreads.items():
        noise = np.random.default_rng([zlib.crc32(name.encode()), seed]).standard_normal(out[name].shape)
        drawn = base * np.exp(spread * noise) if base else spread * noise
        out[name] = jnp.asarray(drawn.astype(out[name].dtype))
    for name, factor in factors.items():
        out[name] = (out[name] * factor).astype(out[name].dtype)
    return out
```

```python
from contextlib import ExitStack

import concourse.bass as bass
from concourse import mybir

ALU = mybir.AluOpType
ACT = mybir.ActivationFunctionType
AX = mybir.AxisListType
F32 = mybir.dt.float32
F32R = mybir.dt.float32r

P = 128
N_IMG, C, HW = 8, 512, 1024
HEADS = 8
D = C // HEADS
CT = C // P
ST = HW // P
NCH = HW // 512
STEPS = HEADS * ST
GE = 160
TAIL = GE - P
SEL = 112
NF = 32
ROUND = 12582912.0
QSCALE = 1.0 / 8.0


def f32(ap):
    return ap.bitcast(F32)


def build(nc, x, wqk, bqk, wv, wo, bv, bo_rep, w0, w0mask, w1, w2, ident_d, ramp_d, iota_d, out):
    ctx = ExitStack()
    with ctx:
        def sb(name, shape, dt=F32, c=ctx):
            return c.enter_context(nc.sbuf_tensor(name, shape, dt))

        def ps(name, shape, c, dt=F32):
            return c.enter_context(nc.psum_tensor(name, shape, dt))

        def sem(name):
            return ctx.enter_context(nc.semaphore(name))

        wqk_s = nc.dram_tensor("wqk_split", (HEADS, P, 2, CT * P), F32, kind="Internal").ap()
        wv_s = nc.dram_tensor("wv_split", (P, 2, CT * C), F32, kind="Internal").ap()
        wo_s = nc.dram_tensor("wo_split", (P, 2, CT * C), F32, kind="Internal").ap()

        ident = sb("ident", [P, P])
        b_qk = sb("b_qk", [P, HEADS])
        b_v = sb("b_v", [P, HEADS])
        bo_all = sb("bo_all", [P, C])
        ramp = sb("ramp", [P, ST * 64])
        iota2 = sb("iota2", [P, ST * 32])
        W0 = sb("W0", [NF, 3, P], F32R)
        W1H = sb("W1H", [P, 3, 2 * P], F32R)
        W1L = sb("W1L", [P, 3, 2 * P], F32R)
        W2S = sb("W2S", [P, 2, 8], F32R)
        OT = sb("OT", [P, CT, HW])

        s_prep_in = sem("s_prep_in")
        s_prep_v = sem("s_prep_v")
        s_prep_hi = sem("s_prep_hi")
        s_prep_lo = sem("s_prep_lo")
        s_prep_out = sem("s_prep_out")

        with ExitStack() as pc:
            raw = sb("raw", [P, HEADS * CT * P], F32, pc)
            hi = sb("hi", [P, HEADS * CT * P], F32R, pc)
            lo = sb("lo", [P, HEADS * CT * P], F32R, pc)
            rawv = sb("rawv", [P, CT * C], F32, pc)
            rawo = sb("rawo", [P, CT * C], F32, pc)
            hiv = sb("hiv", [P, 2 * CT * C], F32R, pc)
            lov = sb("lov", [P, 2 * CT * C], F32R, pc)
            w0r = sb("w0r", [NF, 3 * P], F32, pc)
            w0h = sb("w0h", [NF, 3 * P], F32R, pc)
            w0l = sb("w0l", [NF, 3 * P], F32, pc)
            w0m = sb("w0m", [NF, 2], F32, pc)
            w1r = sb("w1r", [P, 3 * 2 * P], F32, pc)
            w2r = sb("w2r", [P, 2, 4], F32, pc)
            loads = [(raw[:, :], wqk), (rawv[:, :], wv), (rawo[:, :], wo), (b_v[D:P, :], bv),
                     (bo_all[:, :], bo_rep), (ident[:, :], ident_d), (b_qk[:, :], bqk), (ramp[:, :], ramp_d),
                     (iota2[:, :], iota_d), (w0r[:, :], w0), (w0m[:, :], w0mask), (w1r[:, :], w1),
                     (w2r[:, :, :], w2)]
            raw_q = raw[:, :].rearrange("p (a b) -> p a b", b=P)[:, :, 0:D]
            with nc.Block() as block:
                @block.sync
                def _(sp):
                    for dst, src in loads:
                        sp.dma_start(dst, src).then_inc(s_prep_in, 16)
                    sp.wait_ge(s_prep_hi, 3)
                    sp.wait_ge(s_prep_lo, 3)
                    for h in range(HEADS):
                        sp.dma_start(wqk_s[h, :, 0, :], f32(hi[:, h * C:(h + 1) * C])).then_inc(s_prep_out, 16)
                        sp.dma_start(wqk_s[h, :, 1, :], f32(lo[:, h * C:(h + 1) * C])).then_inc(s_prep_out, 16)
                    for n, dst in enumerate((wv_s, wo_s)):
                        cols = slice(n * CT * C, (n + 1) * CT * C)
                        sp.dma_start(dst[:, 0, :], f32(hiv[:, cols])).then_inc(s_prep_out, 16)
                        sp.dma_start(dst[:, 1, :], f32(lov[:, cols])).then_inc(s_prep_out, 16)
                    sp.wait_ge(s_prep_out, 16 * (2 * HEADS + 4))

                @block.scalar
                def _(act):
                    act.wait_ge(s_prep_in, 16 * len(loads))
                    act.wait_ge(s_prep_v, 1)
                    act.activation(hi[:, :], raw[:, :], ACT.Copy).then_inc(s_prep_hi, 1)
                    act.activation(hiv[:, 0:CT * C], rawv[:, :], ACT.Copy).then_inc(s_prep_hi, 1)
                    act.activation(hiv[:, CT * C:], rawo[:, :], ACT.Copy).then_inc(s_prep_hi, 1)
                    act.activation(w0h[:, :], w0r[:, :], ACT.Copy).then_inc(s_prep_hi, 1)
                    act.activation(W1H[:, :, :].rearrange("p a b -> p (a b)"), w1r[:, :], ACT.Copy)\
                       .then_inc(s_prep_hi, 1)
                    act.activation(W2S[:, :, 0:4], w2r[:, :, :], ACT.Copy).then_inc(s_prep_hi, 1)

                @block.vector
                def _(dve):
                    dve.wait_ge(s_prep_in, 16 * len(loads))
                    dve.tensor_scalar(raw_q, raw_q, QSCALE, None, ALU.mult).then_inc(s_prep_v, 1)
                    dve.tensor_scalar(b_qk[0:D, :], b_qk[0:D, :], QSCALE, None, ALU.mult).then_inc(s_prep_v, 1)
                    dve.wait_ge(s_prep_v, 1)
                    dve.wait_ge(s_prep_hi, 1)
                    dve.tensor_tensor(lo[:, :], raw[:, :], f32(hi[:, :]), ALU.subtract).then_inc(s_prep_lo, 1)
                    dve.wait_ge(s_prep_hi, 3)
                    dve.tensor_tensor(lov[:, 0:CT * C], rawv[:, :], f32(hiv[:, 0:CT * C]), ALU.subtract)\
                       .then_inc(s_prep_lo, 1)
                    dve.tensor_tensor(lov[:, CT * C:], rawo[:, :], f32(hiv[:, CT * C:]), ALU.subtract)\
                       .then_inc(s_prep_lo, 1)
                    dve.wait_ge(s_prep_hi, 6)
                    dve.tensor_tensor(W1L[:, :, :].rearrange("p a b -> p (a b)"), w1r[:, :],
                                      f32(W1H[:, :, :].rearrange("p a b -> p (a b)")), ALU.subtract)
                    dve.tensor_tensor(W2S[:, :, 4:8], w2r[:, :, :], f32(W2S[:, :, 0:4]), ALU.subtract)
                    dve.tensor_tensor(w0l[:, :], w0r[:, :], f32(w0h[:, :]), ALU.subtract).then_inc(s_prep_v, 1)
                    dve.wait_ge(s_prep_v, 3)
                    dve.tensor_scalar(w0l[:, :], w0l[:, :], w0m[:, 1:2], None, ALU.mult).then_inc(s_prep_v, 1)
                    dve.wait_ge(s_prep_v, 4)
                    dve.scalar_tensor_tensor(out=W0[:, :, :].rearrange("p a b -> p (a b)"), in0=f32(w0h[:, :]),
                                             scalar=w0m[:, 0:1], in1=w0l[:, :], op0=ALU.mult, op1=ALU.add)

        names = """f_x f_wv f_wqk f_tok f_copy f_stat f_var f_std f_norm f_back f_hi f_lo f_v f_vhi f_vlo f_qk
                   f_qk_hi f_qk_lo f_kdup
                   a_w0 a_w1 a_scores a_max a_exp a_recip a_norm a_tr a_hi a_lo a_pv a_obot a_o a_proj a_proj_hi
                   a_proj_lo a_kdup
                   b_x b_wo b_bias b_ohi b_olo b_y b_res b_tok b_copy b_stat b_var b_std b_sel b_scale b_vec b_feat
                   b_ft b_ftc b_l0 b_h1hi b_h1lo b_l1 b_h2hi b_h2lo b_l2 b_add b_back b_out b_store""".split()
        S = {n: sem(n) for n in names}
        nums = sorted(s.num for s in S.values())
        assert nums == list(range(nums[0], nums[0] + len(nums)))

        xv = x.rearrange("n (t p) s -> n p t s", p=P)
        ov = out.rearrange("n (t p) s -> n p t s", p=P)

        with nc.Fori(0, N_IMG) as img:
            with ExitStack() as ac:
                XH = sb("XH", [P, CT, HW], F32R, ac)
                XL = sb("XL", [P, CT, HW], F32R, ac)
                VS = sb("VS", [P, ST, HEADS, 2 * D], F32R, ac)
                QS = [sb(f"QS{i}", [P, HW], F32R, ac) for i in range(2)]
                KH = [sb(f"KH{i}", [P, HW], F32R, ac) for i in range(2)]
                KL = [sb(f"KL{i}", [P, HW], F32R, ac) for i in range(2)]
                WQ = [sb(f"WQ{i}", [P, 2, CT, P], F32R, ac) for i in range(2)]
                front(nc, S, img, xv, wv_s, wqk_s, ident, b_qk, XH, XL, VS, QS, KH, KL, WQ)
                attention(nc, S, wqk_s, ident, b_qk, b_v, XH, XL, VS, QS, KH, KL, WQ, OT)
            back(nc, S, img, xv, ov, wo_s, ident, bo_all, ramp, iota2, W0, W1H, W1L, W2S, OT)
            nc.all_engine_barrier(sems_to_clear=range(nums[0], nums[-1] + 1))


def qk_project(pe, bank, W, XH, XL, chunk, part=(0, 12)):
    passes = [(w, xx, k) for w, xx in ((0, XH), (1, XH), (0, XL)) for k in range(CT)]
    for n in range(*part):
        w, xx, k = passes[n]
        mm = pe.matmul(bank, W[:, w, k, :], xx[:, k, chunk * 512:(chunk + 1) * 512],
                       start=(n == 0), stop=(n == len(passes) - 1))
    return mm


def rstd_of(dve, S, s_done, s_std, var, std, r, tmp, nb, mean, eps_var, base):
    n = base

    def step(ins):
        nonlocal n
        ins.then_inc(s_done, 1)
        n += 1
        dve.wait_ge(s_done, n)

    dve.wait_ge(s_std, 1)
    step(dve.reciprocal(r, std))
    step(dve.tensor_tensor(tmp, r, r, ALU.mult))
    step(dve.tensor_tensor(tmp, tmp, eps_var, ALU.mult))
    step(dve.tensor_scalar(tmp, tmp, -0.5, 1.5, ALU.mult, ALU.add))
    step(dve.tensor_tensor(r, r, tmp, ALU.mult))
    step(dve.scalar_tensor_tensor(out=nb, in0=mean, scalar=-1.0, in1=r, op0=ALU.mult, op1=ALU.mult))
    return n


def front(nc, S, img, xv, wv_s, wqk_s, ident, b_qk, XH, XL, VS, QS, KH, KL, WQ):
    with ExitStack() as c:
        def sb(name, shape, dt=F32):
            return c.enter_context(nc.sbuf_tensor(name, shape, dt))

        def bank(name):
            return c.enter_context(nc.psum_tensor(name, [P, 512], F32))

        X = sb("X", [P, CT, HW])
        XT = sb("XT", [P, ST, C])
        WV = sb("WV", [P, 2, CT, C], F32R)
        stats = sb("f_stats", [P, ST, 6])
        mv = sb("f_mv", [P, ST, 2])
        ev = sb("f_ev", [P, ST])
        std = sb("f_stdt", [P, ST])
        r = sb("f_r", [P, ST])
        tmp = sb("f_tmp", [P, ST])
        nb = sb("f_nb", [P, ST])
        pt = [bank(f"f_pt{i}") for i in range(3)]
        pv = [bank(f"f_pv{i}") for i in range(3)]
        pq = [bank(f"f_pq{i}") for i in range(2)]
        block = c.enter_context(nc.Block())

        @block.sync
        def _(sp):
            for t in range(CT):
                sp.dma_start(X[:, t, :], xv[img, :, t, :]).then_inc(S["f_x"], 16)
            sp.dma_start(f32(WV[:, :, :, :].rearrange("p a k n -> p a (k n)")), wv_s).then_inc(S["f_wv"], 16)
            for h in range(2):
                sp.dma_start(f32(WQ[h][:, :, :, :].rearrange("p a k n -> p a (k n)")), wqk_s[h])\
                  .then_inc(S["f_wqk"], 16)
            sp.wait_ge(S["f_qk_lo"], NCH)
            sp.dma_start(f32(KH[0][0:D, :]), f32(KH[0][D:P, :])).then_inc(S["f_kdup"], 16)
            sp.dma_start(f32(KL[0][0:D, :]), f32(KL[0][D:P, :])).then_inc(S["f_kdup"], 16)
            sp.wait_ge(S["f_kdup"], 32)

        @block.tensor
        def _(pe):
            pe.wait_ge(S["f_x"], 16 * CT)
            for s in range(ST):
                if s >= 3:
                    pe.wait_ge(S["f_copy"], s - 2)
                for t in range(CT):
                    mm = pe.transpose(pt[s % 3][:, t * P:(t + 1) * P], X[:, t, s * P:(s + 1) * P], ident[:, :])
                mm.then_inc(S["f_tok"], 1)
            pe.wait_ge(S["f_copy"], ST)
            for s in range(ST):
                pe.wait_ge(S["f_norm"], s + 1)
                if s >= 3:
                    pe.wait_ge(S["f_lo"], s - 2)
                for t in range(CT):
                    mm = pe.transpose(pt[s % 3][:, t * P:(t + 1) * P], XT[:, s, t * P:(t + 1) * P], ident[:, :])
                mm.then_inc(S["f_back"], 1)
            pe.wait_ge(S["f_wv"], 16)
            for s in range(ST):
                pe.wait_ge(S["f_lo"], s + 1)
                if s >= 3:
                    pe.wait_ge(S["f_vlo"], s - 2)
                passes = [(xx, w, k) for xx, w in ((XH, 0), (XL, 0), (XH, 1)) for k in range(CT)]
                for n, (xx, w, k) in enumerate(passes):
                    mm = pe.matmul(pv[s % 3][:, :], xx[:, k, s * P:(s + 1) * P], WV[:, w, k, :],
                                   start=(n == 0), stop=(n == len(passes) - 1))
                mm.then_inc(S["f_v"], 1)
            pe.wait_ge(S["f_wqk"], 32)
            for n in range(NCH):
                qk_project(pe, pq[n][:, :], WQ[0], XH, XL, n).then_inc(S["f_qk"], 1)

        @block.scalar
        def _(act):
            for s in range(ST):
                act.wait_ge(S["f_tok"], s + 1)
                act.activation(XT[:, s, :], pt[s % 3][:, :], ACT.Copy).then_inc(S["f_copy"], 1)
            act.wait_ge(S["f_var"], 1)
            act.activation(std[:, :], ev[:, :], ACT.Sqrt).then_inc(S["f_std"], 1)
            for s in range(ST):
                act.wait_ge(S["f_back"], s + 1)
                act.activation(XH[:, :, s * P:(s + 1) * P], pt[s % 3][:, :].rearrange("p (t n) -> p t n", t=CT),
                               ACT.Copy).then_inc(S["f_hi"], 1)
            for s in range(ST):
                act.wait_ge(S["f_v"], s + 1)
                act.activation(VS[:, s, :, 0:D], pv[s % 3][:, :].rearrange("p (h d) -> p h d", h=HEADS),
                               ACT.Copy).then_inc(S["f_vhi"], 1)
            for n in range(NCH):
                cs = slice(n * 512, (n + 1) * 512)
                act.wait_ge(S["f_qk"], n + 1)
                act.activation(QS[0][0:D, cs], pq[n][0:D, :], ACT.Identity, bias=b_qk[0:D, 0:1])
                act.activation(KH[0][D:P, cs], pq[n][D:P, :], ACT.Identity, bias=b_qk[D:P, 0:1])\
                   .then_inc(S["f_qk_hi"], 1)

        @block.vector
        def _(dve):
            for s in range(ST):
                dve.wait_ge(S["f_copy"], s + 1)
                dve.bn_stats(stats[:, s, :], XT[:, s, :]).then_inc(S["f_stat"], 1)
            dve.wait_ge(S["f_stat"], ST)
            for s in range(ST):
                dve.bn_aggr(mv[:, s, :], stats[:, s, :]).then_inc(S["f_stat"], 1)
            dve.wait_ge(S["f_stat"], 2 * ST)
            dve.tensor_scalar(ev[:, :], mv[:, :, 1], 1e-6, None, ALU.add).then_inc(S["f_var"], 1)
            rstd_of(dve, S, S["f_var"], S["f_std"], mv, std[:, :], r[:, :], tmp[:, :], nb[:, :],
                    mv[:, :, 0], ev[:, :], 1)
            for s in range(ST):
                dve.wait_ge(S["f_hi"], s + 1)
                xs = XL[:, :, s * P:(s + 1) * P]
                dve.tensor_tensor(xs, pt[s % 3][:, :].rearrange("p (t n) -> p t n", t=CT),
                                  f32(XH[:, :, s * P:(s + 1) * P]), ALU.subtract).then_inc(S["f_lo"], 1)
            for s in range(ST):
                dve.wait_ge(S["f_vhi"], s + 1)
                dve.tensor_tensor(VS[:, s, :, D:2 * D], pv[s % 3][:, :].rearrange("p (h d) -> p h d", h=HEADS),
                                  f32(VS[:, s, :, 0:D]), ALU.subtract).then_inc(S["f_vlo"], 1)
            for n in range(NCH):
                dve.wait_ge(S["f_qk_hi"], n + 1)
                split_qk(dve, pq[n], QS[0], KH[0], KL[0], b_qk[:, 0:1], n).then_inc(S["f_qk_lo"], 1)

        @block.gpsimd
        def _(pool):
            pool.wait_ge(S["f_var"], 7)
            for s in range(ST):
                pool.tensor_scalar(XT[:, s, :], XT[:, s, :], r[:, s:s + 1], nb[:, s:s + 1], ALU.mult, ALU.add)\
                    .then_inc(S["f_norm"], 1)


def split_qk(dve, bank, QSb, KHb, KLb, bias, n):
    cs = slice(n * 512, (n + 1) * 512)
    dve.scalar_tensor_tensor(out=QSb[D:P, cs], in0=bank[0:D, :], scalar=bias[0:D, :], in1=f32(QSb[0:D, cs]),
                             op0=ALU.add, op1=ALU.subtract)
    return dve.scalar_tensor_tensor(out=KLb[D:P, cs], in0=bank[D:P, :], scalar=bias[D:P, :],
                                    in1=f32(KHb[D:P, cs]), op0=ALU.add, op1=ALU.subtract)


def attention(nc, S, wqk_s, ident, b_qk, b_v, XH, XL, VS, QS, KH, KL, WQ, OT):
    NCK = STEPS // 4

    with ExitStack() as c:
        def sb(name, shape, dt=F32):
            return c.enter_context(nc.sbuf_tensor(name, shape, dt))

        PR = [sb(f"PR{i}", [P, HW]) for i in range(2)]
        PH = [sb(f"PH{i}", [P, ST, 512], F32R) for i in range(2)]
        PL = [sb(f"PL{i}", [P, ST, 512], F32R) for i in range(2)]
        OB = [sb(f"OB{i}", [D, 512]) for i in range(2)]
        nmax = sb("nmax", [P, STEPS])
        rsum = sb("rsum", [P, STEPS])
        rinv = sb("rinv", [P, STEPS])
        pS = [c.enter_context(nc.psum_tensor(f"pS{i}", [P, HW], F32)) for i in range(2)]
        pT = [c.enter_context(nc.psum_tensor(f"pT{i}", [P, 512], F32)) for i in range(2)]
        pJ = c.enter_context(nc.psum_tensor("pJ", [P, 512], F32))
        pO = c.enter_context(nc.psum_tensor("pO", [P, 512], F32))
        block = c.enter_context(nc.Block())

        PROJ = {0: (0, (0, 6)), 1: (0, (6, 12)), 3: (1, (0, 12))}
        EVAC = {2: 0, 4: 1}

        @block.sync
        def _(sp):
            for h in range(1, HEADS):
                if h >= 2:
                    if h >= 3:
                        sp.wait_ge(S["a_proj"], 2 * (h - 2))
                    sp.dma_start(f32(WQ[h % 2][:, :, :, :].rearrange("p a k n -> p a (k n)")), wqk_s[h])\
                      .then_inc(S[f"a_w{h % 2}"], 16)
                sp.wait_ge(S["a_proj_lo"], 2 * h)
                sp.dma_start(f32(KH[h % 2][0:D, :]), f32(KH[h % 2][D:P, :])).then_inc(S["a_kdup"], 16)
                sp.dma_start(f32(KL[h % 2][0:D, :]), f32(KL[h % 2][D:P, :])).then_inc(S["a_kdup"], 16)
            sp.wait_ge(S["a_kdup"], 32 * (HEADS - 1))

        @block.tensor
        def _(pe):
            def scores(g):
                h, t = divmod(g, ST)
                if t == 0 and h > 0:
                    pe.wait_ge(S["a_proj_lo"], 2 * h)
                    pe.wait_ge(S["a_kdup"], 32 * h)
                if g >= 2:
                    pe.wait_ge(S["a_exp"], g - 1)
                q = QS[h % 2][:, t * P:(t + 1) * P]
                for n in range(NCH):
                    cs = slice(n * 512, (n + 1) * 512)
                    pe.matmul(pS[g % 2][:, cs], q, KH[h % 2][:, cs], start=True, stop=False)
                    mm = pe.matmul(pS[g % 2][:, cs], q, KL[h % 2][:, cs], start=False, stop=True)
                mm.then_inc(S["a_scores"], 1)

            def turn(g):
                pe.wait_ge(S["a_norm"], g + 1)
                for half in range(2):
                    if g >= 1:
                        pe.wait_ge(S["a_lo"], 2 * (g - 1) + half + 1)
                    for k in range(4):
                        kb = 4 * half + k
                        mm = pe.transpose(pT[half][:, k * P:(k + 1) * P], PR[g % 2][:, kb * P:(kb + 1) * P],
                                          ident[:, :])
                    mm.then_inc(S["a_tr"], 1)

            def project(h, chunk, part):
                if part[0] == 0:
                    if h >= 2:
                        pe.wait_ge(S[f"a_w{h % 2}"], 16 * (h // 2 if h % 2 == 0 else (h - 1) // 2))
                    if 2 * (h - 1) + chunk > 0:
                        pe.wait_ge(S["a_proj_lo"], 2 * (h - 1) + chunk)
                mm = qk_project(pe, pJ[:, :], WQ[h % 2], XH, XL, chunk, part)
                if part[1] == 12:
                    mm.then_inc(S["a_proj"], 1)

            def values(ck, part):
                h = ck // 2
                if part == 0:
                    pe.wait_ge(S["a_lo"], 8 * (ck + 1))
                    if ck >= 1:
                        pe.wait_ge(S["a_o"], ck)
                for kb in (2 * part, 2 * part + 1):
                    v = VS[:, kb, h, :]
                    pe.matmul(pO[:, :], v, PH[ck % 2][:, kb, :], start=(kb == 0), stop=False)
                    mm = pe.matmul(pO[:, :], v, PL[ck % 2][:, kb, :], start=False, stop=(kb == ST - 1))
                if part == 3:
                    mm.then_inc(S["a_pv"], 1)

            scores(0)
            scores(1)
            for g in range(STEPS + 4):
                h, t = divmod(g, ST)
                if g + 2 < STEPS:
                    scores(g + 2)
                if g < STEPS:
                    turn(g)
                if h + 1 < HEADS and t in PROJ:
                    project(h + 1, *PROJ[t])
                if g >= 4:
                    values(g // 4 - 1, g % 4)

        @block.scalar
        def _(act):
            def exp(g):
                act.wait_ge(S["a_max"], g + 1)
                if g >= 2:
                    act.wait_ge(S["a_tr"], 2 * (g - 1))
                act.activation(PR[g % 2][:, :], pS[g % 2][:, :], ACT.Exp, bias=nmax[:, g:g + 1],
                               accum_out=rsum[:, g:g + 1]).then_inc(S["a_exp"], 1)

            exp(0)
            for g in range(STEPS + 4):
                h, t = divmod(g, ST)
                if g + 1 < STEPS:
                    exp(g + 1)
                if h + 1 < HEADS and t in EVAC:
                    n = EVAC[t]
                    cs = slice(n * 512, (n + 1) * 512)
                    p = (h + 1) % 2
                    act.wait_ge(S["a_proj"], 2 * h + n + 1)
                    act.activation(QS[p][0:D, cs], pJ[0:D, :], ACT.Identity, bias=b_qk[0:D, h + 1:h + 2])
                    act.activation(KH[p][D:P, cs], pJ[D:P, :], ACT.Identity, bias=b_qk[D:P, h + 1:h + 2])\
                       .then_inc(S["a_proj_hi"], 1)
                if g < STEPS:
                    ck = g // 4
                    if ck >= 2:
                        act.wait_ge(S["a_pv"], ck - 1)
                    for half in range(2):
                        act.wait_ge(S["a_tr"], 2 * g + half + 1)
                        act.activation(PH[ck % 2][:, 4 * half:4 * half + 4, (g % 4) * P:(g % 4 + 1) * P],
                                       pT[half][:, :].rearrange("p (k n) -> p k n", k=4), ACT.Copy)\
                           .then_inc(S["a_hi"], 1)
                if g >= 4 and g % 4 == 3:
                    ck = g // 4 - 1
                    act.wait_ge(S["a_pv"], ck + 1)
                    if ck >= 2:
                        act.wait_ge(S["a_o"], ck - 1)
                    act.activation(OB[ck % 2][:, :], pO[D:P, :], ACT.Identity,
                                   bias=b_v[D:P, ck // 2:ck // 2 + 1]).then_inc(S["a_obot"], 1)

        @block.vector
        def _(dve):
            def rowmax(g):
                dve.wait_ge(S["a_scores"], g + 1)
                dve.tensor_reduce(nmax[:, g:g + 1], pS[g % 2][:, :], AX.X, ALU.max, negate=True)\
                   .then_inc(S["a_max"], 1)

            def recip(g):
                dve.wait_ge(S["a_exp"], g + 1)
                dve.reciprocal(rinv[:, g:g + 1], rsum[:, g:g + 1]).then_inc(S["a_recip"], 1)

            rowmax(0)
            rowmax(1)
            recip(0)
            for g in range(STEPS + 4):
                h, t = divmod(g, ST)
                if g + 2 < STEPS:
                    rowmax(g + 2)
                if g + 1 < STEPS:
                    recip(g + 1)
                if h + 1 < HEADS and t in EVAC:
                    p = (h + 1) % 2
                    dve.wait_ge(S["a_proj_hi"], 2 * h + EVAC[t] + 1)
                    split_qk(dve, pJ, QS[p], KH[p], KL[p], b_qk[:, h + 1:h + 2], EVAC[t])\
                        .then_inc(S["a_proj_lo"], 1)
                if g < STEPS:
                    ck = g // 4
                    for half in range(2):
                        ks = slice(4 * half, 4 * half + 4)
                        qs = slice((g % 4) * P, (g % 4 + 1) * P)
                        dve.wait_ge(S["a_hi"], 2 * g + half + 1)
                        dve.tensor_tensor(PL[ck % 2][:, ks, qs], pT[half][:, :].rearrange("p (k n) -> p k n", k=4),
                                          f32(PH[ck % 2][:, ks, qs]), ALU.subtract).then_inc(S["a_lo"], 1)
                if g >= 4 and g % 4 == 3:
                    ck = g // 4 - 1
                    hh, n = divmod(ck, 2)
                    dve.wait_ge(S["a_obot"], ck + 1)
                    by_query = [z.rearrange("d (m jj jp) -> d jp jj m", jp=2, jj=CT) for z in (pO[0:D, :], OB[ck % 2][:, :])]
                    cols = slice(hh * P + n * D, hh * P + (n + 1) * D)
                    for jp in range(2):
                        last = dve.tensor_tensor(OT[jp * D:(jp + 1) * D, :, cols], by_query[0][:, jp], by_query[1][:, jp],
                                                 ALU.add)
                    last.then_inc(S["a_o"], 1)

        @block.gpsimd
        def _(pool):
            for g in range(STEPS):
                pool.wait_ge(S["a_recip"], g + 1)
                pool.tensor_scalar(PR[g % 2][:, :], PR[g % 2][:, :], rinv[:, g:g + 1], 1.0, ALU.mult, ALU.mult)\
                    .then_inc(S["a_norm"], 1)


def back(nc, S, img, xv, ov, wo_s, ident, bo_all, ramp, iota2, W0, W1H, W1L, W2S, OT):
    with ExitStack() as c:
        def sb(name, shape, dt=F32):
            return c.enter_context(nc.sbuf_tensor(name, shape, dt))

        def bank(name):
            return c.enter_context(nc.psum_tensor(name, [P, 512], F32))

        OH = sb("OH", [P, CT, HW], F32R)
        OL = sb("OL", [P, CT, HW], F32R)
        WO = sb("WO", [P, 2, CT, C], F32R)
        X1 = sb("X1", [P, CT, HW])
        TK = sb("TK", [P, ST, C])
        YO = sb("YO", [P, CT, HW])
        XN = sb("XN", [P, ST, SEL])
        stats = sb("b_stats", [P, ST, 6])
        mv = sb("b_mv", [P, ST, 2])
        ev = sb("b_ev", [P, ST])
        std = sb("b_stdt", [P, ST])
        r = sb("b_r", [P, ST])
        r1 = sb("b_r1", [P, ST])
        tmp = sb("b_tmp", [P, ST])
        nb = sb("b_nb", [P, ST])
        first = sb("first", [P, ST, 64])
        idx = sb("idx", [P, ST, 2, 2])
        idx2 = sb("idx2", [P, ST, 2, 2])
        cmp3 = sb("cmp3", [P, ST, 3])
        mask = sb("mask", [P, ST, 2])
        mtmp = sb("mtmp", [P, ST, 2])
        XNR = sb("XNR", [P, ST, 2], F32R)
        XNL = sb("XNL", [P, ST, 2])
        F = sb("F", [P, ST, 2, NF])
        FT = sb("FT", [NF, 2 * HW], F32R)
        H1H = [sb(f"H1H{i}", [P, 3, 512], F32R) for i in range(1)]
        H1L = [sb(f"H1L{i}", [P, 3, 512], F32R) for i in range(1)]
        H2H = [sb(f"H2H{i}", [P, 2, 512], F32R) for i in range(1)]
        H2L = [sb(f"H2L{i}", [P, 2, 512], F32R) for i in range(1)]
        Y8 = sb("Y8", [P, 2 * ST, 8])
        Y4 = sb("Y4", [P, 2 * ST, 4])
        YS = sb("YS", [P, 2, ST, 2])
        YR = sb("YR", [P, 2, ST])
        EQ = sb("EQ", [P, ST, 2, 16])
        CY = sb("CY", [P, ST])
        act_t = sb("act_t", [P, ST])
        pa = [bank(f"b_pa{i}") for i in range(2)]
        ph = [bank(f"b_ph{i}") for i in range(3)]
        pg = [bank(f"b_pg{i}") for i in range(2)]
        py = bank("b_py")
        NQ = 4
        VEC = [0]
        MARK = {}
        block = c.enter_context(nc.Block())

        @block.sync
        def _(sp):
            for t in range(CT):
                sp.dma_start(X1[:, t, :], xv[img, :, t, :]).then_inc(S["b_x"], 16)
            sp.dma_start(f32(WO[:, :, :, :].rearrange("p a k n -> p a (k n)")), wo_s).then_inc(S["b_wo"], 16)
            sp.wait_ge(S["b_out"], ST)
            for t in range(CT):
                sp.dma_start(ov[img, :, t, :], YO[:, t, :]).then_inc(S["b_store"], 16)
            sp.wait_ge(S["b_store"], 16 * CT)

        @block.gpsimd
        def _(pool):
            pool.wait_ge(S["b_x"], 16 * CT)
            for t in range(CT):
                for n in range(NCH):
                    xs = X1[:, t, n * 512:(n + 1) * 512]
                    pool.tensor_tensor(xs, xs, bo_all[:, :], ALU.add).then_inc(S["b_bias"], 1)
            pool.wait_ge(S["b_sel"], 1)
            for s in range(ST):
                pool.tensor_scalar(TK[:, s, :], TK[:, s, :], r1[:, s:s + 1], nb[:, s:s + 1], ALU.mult, ALU.add)\
                    .then_inc(S["b_scale"], 1)

        @block.tensor
        def _(pe):
            pe.wait_ge(S["b_wo"], 16)
            pe.wait_ge(S["b_olo"], CT)
            passes = [(o, w, k) for o, w in ((OH, 0), (OL, 0), (OH, 1)) for k in range(CT)]
            for i in range(CT * NCH):
                t, n = divmod(i, NCH)
                if i >= 2:
                    pe.wait_ge(S["b_res"], i - 1)
                for m, (o, w, k) in enumerate(passes):
                    tok = o[:, k, t * 2 * P:(t + 1) * 2 * P].rearrange("p (c two) -> p c two", two=2)[:, :, n]
                    mm = pe.matmul(pa[i % 2][:, :], tok, WO[:, w, k, :], start=(m == 0), stop=(m == 11))
                mm.then_inc(S["b_y"], 1)
            pe.wait_ge(S["b_res"], CT * NCH)
            for s in range(ST):
                if s >= 2:
                    pe.wait_ge(S["b_copy"], s - 1)
                for t in range(CT):
                    mm = pe.transpose(pa[s % 2][:, t * P:(t + 1) * P], X1[:, t, s * P:(s + 1) * P], ident[:, :])
                mm.then_inc(S["b_tok"], 1)
            pe.wait_ge(S["b_copy"], ST)
            pe.wait_ge(S["b_feat"], 1)
            for q in range(NQ):
                if q >= 2:
                    pe.wait_ge(S["b_ftc"], q - 1)
                for k in range(4):
                    n, s = divmod(4 * q + k, ST)
                    mm = pe.transpose(pa[q % 2][0:NF, k * P:(k + 1) * P], F[:, s, n, :], ident[:, :])
                mm.then_inc(S["b_ft"], 1)
            for q in range(NQ):
                pe.wait_ge(S["b_ftc"], q + 1)
                for m in range(3):
                    if q >= 1:
                        pe.wait_ge(S["b_h1lo"], 3 * (q - 1) + m + 1)
                    pe.matmul(ph[m][:, :], W0[:, m, :], FT[:, q * 512:(q + 1) * 512], start=True, stop=True)\
                      .then_inc(S["b_l0"], 1)
                for m in range(2):
                    if q >= 1:
                        pe.wait_ge(S["b_h2lo"], 2 * (q - 1) + m + 1)
                    i = 0
                    for k in range(3):
                        if m == 0:
                            pe.wait_ge(S["b_h1lo"], 3 * q + k + 1)
                        K = P if k < 2 else 2 * TAIL + 2
                        for w, hh in ((W1H, H1H), (W1L, H1H), (W1H, H1L)):
                            mm = pe.matmul(pg[m][:, :], w[0:K, k, m * P:(m + 1) * P], hh[0][0:K, k, :],
                                           start=(i == 0), stop=(i == 8))
                            i += 1
                    mm.then_inc(S["b_l1"], 1)
                pe.wait_ge(S["b_h2lo"], 2 * (q + 1))
                for k in range(4):
                    j = 4 * q + k
                    ts = slice(k * P, (k + 1) * P)
                    for m in range(2):
                        K = P if m == 0 else TAIL + 2
                        pe.matmul(py[:, 8 * j:8 * j + 8], H2H[0][0:K, m, ts], W2S[0:K, m, :],
                                  start=(m == 0), stop=False)
                        mm = pe.matmul(py[:, 8 * j:8 * j + 8], H2L[0][0:K, m, ts], W2S[0:K, m, :],
                                       start=False, stop=(m == 1))
                mm.then_inc(S["b_l2"], 1)
            for s in range(ST):
                if s == 0:
                    pe.wait_ge(S["b_add"], 1)
                if s >= 2:
                    pe.wait_ge(S["b_out"], s - 1)
                for t in range(CT):
                    mm = pe.transpose(pa[s % 2][:, t * P:(t + 1) * P], TK[:, s, t * P:(t + 1) * P], ident[:, :])
                mm.then_inc(S["b_back"], 1)

        @block.scalar
        def _(act):
            for k in range(CT):
                act.activation(OH[:, k, :], OT[:, k, :], ACT.Copy).then_inc(S["b_ohi"], 1)
            for s in range(ST):
                act.wait_ge(S["b_tok"], s + 1)
                act.activation(TK[:, s, :], pa[s % 2][:, :], ACT.Copy).then_inc(S["b_copy"], 1)
            act.wait_ge(S["b_var"], 1)
            act.activation(std[:, :], ev[:, :], ACT.Sqrt).then_inc(S["b_std"], 1)
            for q in range(NQ):
                act.wait_ge(S["b_ft"], q + 1)
                act.activation(FT[:, q * 512:(q + 1) * 512], pa[q % 2][0:NF, :], ACT.Copy).then_inc(S["b_ftc"], 1)
            for q in range(NQ):
                for m in range(3):
                    act.wait_ge(S["b_l0"], 3 * q + m + 1)
                    if q >= 1 and m == 0:
                        act.wait_ge(S["b_l1"], 2 * q)
                    act.activation(H1H[0][:, m, :], ph[m][:, :], ACT.Relu).then_inc(S["b_h1hi"], 1)
                for m in range(2):
                    act.wait_ge(S["b_l1"], 2 * q + m + 1)
                    if q >= 1 and m == 0:
                        act.wait_ge(S["b_l2"], q)
                    act.activation(H2H[0][:, m, :], pg[m][:, :], ACT.Relu).then_inc(S["b_h2hi"], 1)
            for s in range(ST):
                act.wait_ge(S["b_back"], s + 1)
                act.activation(YO[:, :, s * P:(s + 1) * P], pa[s % 2][:, :].rearrange("p (t n) -> p t n", t=CT),
                               ACT.Copy).then_inc(S["b_out"], 1)

        @block.vector
        def _(dve):
            n = [0]

            def step(ins):
                ins.then_inc(S["b_vec"], 1)
                n[0] += 1
                dve.wait_ge(S["b_vec"], n[0])

            for k in range(CT):
                dve.wait_ge(S["b_ohi"], k + 1)
                dve.tensor_tensor(OL[:, k, :], OT[:, k, :], f32(OH[:, k, :]), ALU.subtract)\
                   .then_inc(S["b_olo"], 1)
            step(dve.memset(F[:, :, :, :], 0.0))
            for i in range(CT * NCH):
                t, m = divmod(i, NCH)
                xs = X1[:, t, m * 512:(m + 1) * 512]
                dve.wait_ge(S["b_y"], i + 1)
                dve.wait_ge(S["b_bias"], i + 1)
                dve.tensor_tensor(xs, pa[i % 2][:, :], xs, ALU.add).then_inc(S["b_res"], 1)
            for s in range(ST):
                dve.wait_ge(S["b_copy"], s + 1)
                dve.bn_stats(stats[:, s, :], TK[:, s, :]).then_inc(S["b_stat"], 1)
            dve.wait_ge(S["b_stat"], ST)
            for s in range(ST):
                dve.bn_aggr(mv[:, s, :], stats[:, s, :]).then_inc(S["b_stat"], 1)
            dve.wait_ge(S["b_stat"], 2 * ST)
            dve.tensor_scalar(ev[:, :], mv[:, :, 1], 1e-5, None, ALU.add).then_inc(S["b_var"], 1)
            rstd_of(dve, S, S["b_var"], S["b_std"], mv, std[:, :], r[:, :], tmp[:, :], nb[:, :],
                    mv[:, :, 0], ev[:, :], 1)
            step(dve.tensor_scalar(r1[:, :], r[:, :], 1.0, None, ALU.add))
            for s in range(ST):
                last = dve.tensor_scalar(XN[:, s, :], TK[:, s, 0:SEL], r[:, s:s + 1], nb[:, s:s + 1],
                                         ALU.mult, ALU.add)
            last.then_inc(S["b_sel"], 1)
            dve.wait_ge(S["b_sel"], 1)
            step(dve.scalar_tensor_tensor(out=first[:, :, :], in0=XN[:, :, 16:80], scalar=0.5,
                                          in1=ramp[:, :].rearrange("p (s k) -> p s k", s=ST),
                                          op0=ALU.is_gt, op1=ALU.mult))
            step(dve.tensor_reduce(idx[:, :, :, :].rearrange("p s a b -> p (s a b)"),
                                   first[:, :, :].rearrange("p s (g k) -> p (s g) k", k=16), AX.X, ALU.max))
            flat = [z[:, :, :, :].rearrange("p s a b -> p (s a b)") for z in (idx, idx2)]
            step(dve.tensor_scalar(flat[1], flat[0], -1.0, 16.0, ALU.mult, ALU.add))
            step(dve.scalar_tensor_tensor(out=flat[1], in0=flat[0], scalar=0.5, in1=flat[1],
                                          op0=ALU.is_gt, op1=ALU.mult))
            step(dve.tensor_scalar(cmp3[:, :, :], XN[:, :, 0:3], 0.5, None, ALU.is_gt))
            step(dve.tensor_tensor(mask[:, :, 0], cmp3[:, :, 0], cmp3[:, :, 1], ALU.mult))
            step(dve.tensor_tensor(mtmp[:, :, 0], cmp3[:, :, 0], cmp3[:, :, 2], ALU.mult))
            step(dve.tensor_scalar(mtmp[:, :, 1], cmp3[:, :, 1], -1.0, 1.0, ALU.mult, ALU.add))
            step(dve.tensor_tensor(mask[:, :, 1], mtmp[:, :, 0], mtmp[:, :, 1], ALU.mult))
            step(dve.tensor_tensor(act_t[:, :], mask[:, :, 0], mask[:, :, 1], ALU.add))
            step(dve.tensor_copy(XNR[:, :, :], XN[:, :, 105:107]))
            step(dve.tensor_tensor(XNL[:, :, :], XN[:, :, 105:107], f32(XNR[:, :, :]), ALU.subtract))
            for nib in range(2):
                for net in range(2):
                    mk = mask[:, :, net]
                    for base in (5 * net, 10 + 5 * net):
                        for o in range(2):
                            dve.tensor_tensor(F[:, :, nib, base + o], idx2[:, :, o, nib], mk, ALU.mult)
                            dve.tensor_tensor(F[:, :, nib, base + 2 + o], f32(XNR[:, :, o]), mk, ALU.mult)
                        dve.tensor_copy(F[:, :, nib, base + 4], mk)
                    for base in (20 + 2 * net, 24 + 2 * net):
                        for o in range(2):
                            last = dve.tensor_tensor(F[:, :, nib, base + o], XNL[:, :, o], mk, ALU.mult)
            last.then_inc(S["b_feat"], 1)
            for q in range(NQ):
                for m in range(3):
                    dve.wait_ge(S["b_h1hi"], 3 * q + m + 1)
                    dve.scalar_tensor_tensor(out=H1L[0][:, m, :], in0=ph[m][:, :], scalar=0.0,
                                             in1=f32(H1H[0][:, m, :]), op0=ALU.max, op1=ALU.subtract)\
                       .then_inc(S["b_h1lo"], 1)
                for m in range(2):
                    dve.wait_ge(S["b_h2hi"], 2 * q + m + 1)
                    dve.scalar_tensor_tensor(out=H2L[0][:, m, :], in0=pg[m][:, :], scalar=0.0,
                                             in1=f32(H2H[0][:, m, :]), op0=ALU.max, op1=ALU.subtract)\
                       .then_inc(S["b_h2lo"], 1)
            dve.wait_ge(S["b_l2"], NQ)
            step(dve.tensor_copy(Y8[:, :, :].rearrange("p j k -> p (j k)"), py[:, 0:16 * ST]))
            step(dve.tensor_tensor(Y4[:, :, :], Y8[:, :, 0:4], Y8[:, :, 4:8], ALU.add))
            for nib in range(2):
                for net in range(2):
                    y = Y4[:, nib * ST:(nib + 1) * ST, :].rearrange("p s (v e) -> p s v e", e=2)
                    for v in range(2):
                        last = dve.tensor_tensor(y[:, :, v, net], y[:, :, v, net], mask[:, :, net], ALU.mult)
            step(last)
            for nib in range(2):
                y = Y4[:, nib * ST:(nib + 1) * ST, :].rearrange("p s (v e) -> p s v e", e=2)
                last = dve.tensor_tensor(YS[:, nib, :, :], y[:, :, :, 0], y[:, :, :, 1], ALU.add)
            step(last)
            step(dve.tensor_scalar(YR[:, :, :], YS[:, :, :, 0], -1.0, 16.0, ALU.max, ALU.min))
            step(dve.tensor_scalar(YR[:, :, :], YR[:, :, :], ROUND, None, ALU.add))
            step(dve.tensor_scalar(YR[:, :, :], YR[:, :, :], ROUND, None, ALU.subtract))
            step(dve.tensor_scalar(YR[:, :, :], YR[:, :, :], 0.0, 15.0, ALU.max, ALU.min))
            step(dve.tensor_scalar(YR[:, :, :], YR[:, :, :], 1.0, None, ALU.add))
            for nib in range(2):
                last = dve.tensor_tensor(YR[:, nib, :], YR[:, nib, :], act_t[:, :], ALU.mult)
            step(last)
            step(dve.tensor_scalar(YR[:, :, :], YR[:, :, :], -1.0, None, ALU.add))
            for nib in range(2):
                i16 = iota2[:, :].rearrange("p (s n k) -> p s n k", s=ST, n=2)[:, :, nib, :]
                for s in range(ST):
                    last = dve.tensor_scalar(EQ[:, s, nib, :], i16[:, s, :], YR[:, nib, s:s + 1], 2.0,
                                             ALU.is_equal, ALU.mult)
            step(last)
            step(dve.tensor_scalar(CY[:, :], YS[:, 1, :, 1], 0.5, None, ALU.is_gt))
            dve.wait_ge(S["b_scale"], ST)
            dve.tensor_tensor(TK[:, :, 128:160], TK[:, :, 128:160], EQ[:, :, :, :].rearrange("p s n k -> p s (n k)"),
                              ALU.add)
            dve.tensor_tensor(TK[:, :, 160], TK[:, :, 160], CY[:, :], ALU.add).then_inc(S["b_add"], 1)


def kernel(x, L0_conv_Wq, L0_conv_bq, L0_conv_Wk, L0_conv_bk, L0_conv_Wv, L0_conv_bv, L0_conv_Wo, L0_conv_bo,
           L0_ffn_Wa, L0_ffn_ba, L0_ffn_Ws, L0_ffn_bs):
    import numpy as np
    import concourse.bacc as bacc
    from concourse.bass_utils import run_bass_kernel_spmd

    f = np.float32
    x, wq, bq, wk, bk, wv, bv, wo, bo, wa, ba, ws, bs = [
        np.asarray(a) for a in (x, L0_conv_Wq, L0_conv_bq, L0_conv_Wk, L0_conv_bk, L0_conv_Wv, L0_conv_bv,
                                L0_conv_Wo, L0_conv_bo, L0_ffn_Wa, L0_ffn_ba, L0_ffn_Ws, L0_ffn_bs)]

    def by_channel(w):
        return w.T.reshape(CT, P, -1).transpose(1, 0, 2)

    q4, k4 = (by_channel(w).reshape(P, CT, HEADS, D).transpose(0, 2, 1, 3) for w in (wq, wk))
    wqk = np.concatenate([q4, k4], axis=3).reshape(P, -1)
    bqk = np.concatenate([bq.reshape(HEADS, D).T, bk.reshape(HEADS, D).T], axis=0)

    w0 = np.zeros((NF, 3, P), f)
    for net, (w, b) in enumerate(((wa, ba), (ws, bs))):
        cols = [w[0][:, i] for i in (0, 1, 35, 36)] + [b[0]]
        rows = [(5 * net + i, i) for i in range(5)] + [(10 + 5 * net + i, i) for i in range(5)]
        rows += [(20 + 2 * net + i, 2 + i) for i in range(2)] + [(24 + 2 * net + i, 2 + i) for i in range(2)]
        for row, i in rows:
            w0[row, net, :] = cols[i][0:P]
            w0[row, 2, net * TAIL:(net + 1) * TAIL] = cols[i][P:GE]
            if i == 4:
                w0[row, 2, 2 * TAIL + net] = 1.0
    takes_hi = np.array([1] * 10 + [0] * 10 + [1] * 4 + [0] * 8, f)
    w0mask = np.stack([takes_hi, 1 - takes_hi], axis=1)
    w1 = np.zeros((P, 3, 2, P), f)
    w2 = np.zeros((P, 2, 4), f)
    for net, (w, b) in enumerate(((wa, ba), (ws, bs))):
        wt = w[1].T
        for m, (o0, o1) in enumerate(((0, P), (P, GE))):
            w1[:, net, m, 0:o1 - o0] = wt[0:P, o0:o1]
            w1[net * TAIL:(net + 1) * TAIL, 2, m, 0:o1 - o0] = wt[P:GE, o0:o1]
            w1[2 * TAIL + net, 2, m, 0:o1 - o0] = b[1][o0:o1]
        w1[2 * TAIL + net, 2, 1, TAIL + net] = 1.0
        for v, o in enumerate((100, 101)):
            w2[:, 0, 2 * v + net] = w[2][o, 0:P]
            w2[0:TAIL, 1, 2 * v + net] = w[2][o, P:GE]
            w2[TAIL + net, 1, 2 * v + net] = b[2][o]

    arrays = {
        "x": x.reshape(N_IMG, C, HW),
        "wqk": wqk,
        "bqk": bqk,
        "wv": by_channel(wv).reshape(P, -1),
        "wo": by_channel(wo).reshape(P, -1),
        "bv": bv.reshape(HEADS, D).T,
        "bo_rep": np.repeat(bo[None, :], P, axis=0),
        "w0": w0.reshape(NF, -1),
        "w0mask": w0mask,
        "w1": w1.reshape(P, -1),
        "w2": w2,
        "ident": np.eye(P, dtype=f),
        "ramp": np.tile(np.tile(np.arange(16, 0, -1, dtype=f), 4)[None, :], (P, ST)),
        "iota": np.tile(np.tile(np.arange(16, dtype=f), 2)[None, :], (P, ST)),
    }
    arrays = {"in_" + k: np.ascontiguousarray(v) for k, v in arrays.items()}
    nc = bacc.Bacc("TRN2", target_bir_lowering=False, num_devices=1)
    aps = [nc.dram_tensor(k, v.shape, mybir.dt.from_np(v.dtype), kind="ExternalInput").ap()
           for k, v in arrays.items()]
    out = nc.dram_tensor("out_0", (N_IMG, C, HW), F32, kind="ExternalOutput").ap()
    build(nc, *aps, out)
    r = run_bass_kernel_spmd(nc, [arrays], core_ids=[0])
    return r.results[0]["out_0"].reshape(N_IMG, C, 32, 32)
```

```python
from contextlib import ExitStack

import concourse.bass as bass
from concourse import mybir

ALU = mybir.AluOpType
ACT = mybir.ActivationFunctionType
AX = mybir.AxisListType
F32 = mybir.dt.float32
F32R = mybir.dt.float32r

P = 128
N_IMG, C, HW = 8, 512, 1024
HEADS = 8
D = C // HEADS
CT = C // P
ST = HW // P
NCH = HW // 512
STEPS = HEADS * ST
GE = 160
TAIL = GE - P
SEL = 112
NF = 32
ROUND = 12582912.0
QSCALE = 1.0 / 8.0


def f32(ap):
    return ap.bitcast(F32)


def build(nc, x, wqk, bqk, wv, wo, bv, bo_rep, w0, w0mask, w1, w2, ident_d, ramp_d, iota_d, out):
    ctx = ExitStack()
    with ctx:
        def sb(name, shape, dt=F32, c=ctx):
            return c.enter_context(nc.sbuf_tensor(name, shape, dt))

        def ps(name, shape, c, dt=F32):
            return c.enter_context(nc.psum_tensor(name, shape, dt))

        def sem(name):
            return ctx.enter_context(nc.semaphore(name))

        wqk_s = nc.dram_tensor("wqk_split", (HEADS, P, 2, CT * P), F32, kind="Internal").ap()
        wv_s = nc.dram_tensor("wv_split", (P, 2, CT * C), F32, kind="Internal").ap()
        wo_s = nc.dram_tensor("wo_split", (P, 2, CT * C), F32, kind="Internal").ap()

        ident = sb("ident", [P, P])
        b_qk = sb("b_qk", [P, HEADS])
        b_v = sb("b_v", [P, HEADS])
        bo_all = sb("bo_all", [P, C])
        ramp = sb("ramp", [P, 16])
        iota = sb("iota", [P, 16])
        W0 = sb("W0", [NF, 3, P], F32R)
        W1H = sb("W1H", [P, 3, 2 * P], F32R)
        W1L = sb("W1L", [P, 3, 2 * P], F32R)
        W2S = sb("W2S", [P, 2, 8], F32R)
        OT = sb("OT", [P, CT, HW])

        s_prep_in = sem("s_prep_in")
        s_prep_v = sem("s_prep_v")
        s_prep_hi = sem("s_prep_hi")
        s_prep_lo = sem("s_prep_lo")
        s_prep_out = sem("s_prep_out")

        with ExitStack() as pc:
            raw = sb("raw", [P, HEADS * CT * P], F32, pc)
            hi = sb("hi", [P, HEADS * CT * P], F32R, pc)
            lo = sb("lo", [P, HEADS * CT * P], F32R, pc)
            rawv = sb("rawv", [P, CT * C], F32, pc)
            rawo = sb("rawo", [P, CT * C], F32, pc)
            hiv = sb("hiv", [P, 2 * CT * C], F32R, pc)
            lov = sb("lov", [P, 2 * CT * C], F32R, pc)
            w0r = sb("w0r", [NF, 3 * P], F32, pc)
            w0h = sb("w0h", [NF, 3 * P], F32R, pc)
            w0l = sb("w0l", [NF, 3 * P], F32, pc)
            w0m = sb("w0m", [NF, 2], F32, pc)
            w1r = sb("w1r", [P, 3 * 2 * P], F32, pc)
            w2r = sb("w2r", [P, 2, 4], F32, pc)
            loads = [(raw[:, :], wqk), (rawv[:, :], wv), (rawo[:, :], wo), (b_v[D:P, :], bv),
                     (bo_all[:, :], bo_rep), (ident[:, :], ident_d), (b_qk[:, :], bqk), (ramp[:, :], ramp_d),
                     (iota[:, :], iota_d), (w0r[:, :], w0), (w0m[:, :], w0mask), (w1r[:, :], w1),
                     (w2r[:, :, :], w2)]
            raw_q = raw[:, :].rearrange("p (a b) -> p a b", b=P)[:, :, 0:D]
            with nc.Block() as block:
                @block.sync
                def _(sp):
                    for dst, src in loads:
                        sp.dma_start(dst, src).then_inc(s_prep_in, 16)
                    sp.wait_ge(s_prep_hi, 3)
                    sp.wait_ge(s_prep_lo, 3)
                    for h in range(HEADS):
                        sp.dma_start(wqk_s[h, :, 0, :], f32(hi[:, h * C:(h + 1) * C])).then_inc(s_prep_out, 16)
                        sp.dma_start(wqk_s[h, :, 1, :], f32(lo[:, h * C:(h + 1) * C])).then_inc(s_prep_out, 16)
                    for n, dst in enumerate((wv_s, wo_s)):
                        cols = slice(n * CT * C, (n + 1) * CT * C)
                        sp.dma_start(dst[:, 0, :], f32(hiv[:, cols])).then_inc(s_prep_out, 16)
                        sp.dma_start(dst[:, 1, :], f32(lov[:, cols])).then_inc(s_prep_out, 16)
                    sp.wait_ge(s_prep_out, 16 * (2 * HEADS + 4))

                @block.scalar
                def _(act):
                    act.wait_ge(s_prep_in, 16 * len(loads))
                    act.wait_ge(s_prep_v, 1)
                    act.activation(hi[:, :], raw[:, :], ACT.Copy).then_inc(s_prep_hi, 1)
                    act.activation(hiv[:, 0:CT * C], rawv[:, :], ACT.Copy).then_inc(s_prep_hi, 1)
                    act.activation(hiv[:, CT * C:], rawo[:, :], ACT.Copy).then_inc(s_prep_hi, 1)
                    act.activation(w0h[:, :], w0r[:, :], ACT.Copy).then_inc(s_prep_hi, 1)
                    act.activation(W1H[:, :, :].rearrange("p a b -> p (a b)"), w1r[:, :], ACT.Copy)\
                       .then_inc(s_prep_hi, 1)
                    act.activation(W2S[:, :, 0:4], w2r[:, :, :], ACT.Copy).then_inc(s_prep_hi, 1)

                @block.vector
                def _(dve):
                    dve.wait_ge(s_prep_in, 16 * len(loads))
                    dve.tensor_scalar(raw_q, raw_q, QSCALE, None, ALU.mult).then_inc(s_prep_v, 1)
                    dve.tensor_scalar(b_qk[0:D, :], b_qk[0:D, :], QSCALE, None, ALU.mult).then_inc(s_prep_v, 1)
                    dve.wait_ge(s_prep_v, 1)
                    dve.wait_ge(s_prep_hi, 1)
                    dve.tensor_tensor(lo[:, :], raw[:, :], f32(hi[:, :]), ALU.subtract).then_inc(s_prep_lo, 1)
                    dve.wait_ge(s_prep_hi, 3)
                    dve.tensor_tensor(lov[:, 0:CT * C], rawv[:, :], f32(hiv[:, 0:CT * C]), ALU.subtract)\
                       .then_inc(s_prep_lo, 1)
                    dve.tensor_tensor(lov[:, CT * C:], rawo[:, :], f32(hiv[:, CT * C:]), ALU.subtract)\
                       .then_inc(s_prep_lo, 1)
                    dve.wait_ge(s_prep_hi, 6)
                    dve.tensor_tensor(W1L[:, :, :].rearrange("p a b -> p (a b)"), w1r[:, :],
                                      f32(W1H[:, :, :].rearrange("p a b -> p (a b)")), ALU.subtract)
                    dve.tensor_tensor(W2S[:, :, 4:8], w2r[:, :, :], f32(W2S[:, :, 0:4]), ALU.subtract)
                    dve.tensor_tensor(w0l[:, :], w0r[:, :], f32(w0h[:, :]), ALU.subtract).then_inc(s_prep_v, 1)
                    dve.wait_ge(s_prep_v, 3)
                    dve.tensor_scalar(w0l[:, :], w0l[:, :], w0m[:, 1:2], None, ALU.mult).then_inc(s_prep_v, 1)
                    dve.wait_ge(s_prep_v, 4)
                    dve.scalar_tensor_tensor(out=W0[:, :, :].rearrange("p a b -> p (a b)"), in0=f32(w0h[:, :]),
                                             scalar=w0m[:, 0:1], in1=w0l[:, :], op0=ALU.mult, op1=ALU.add)

        names = """f_x f_wv f_wqk0 f_wqk1 f_tok f_copy f_stat f_var f_std f_norm f_back f_hi f_lo f_v f_vhi f_vlo
                   f_qk f_qk_hi f_qk_lo f_kdup
                   a_w0 a_w1 a_scores a_max a_exp a_recip a_norm a_tr a_hi a_lo a_pv a_obot a_o a_proj a_proj_out a_proj_hi
                   a_proj_lo a_qk
                   b_x0 b_x b_wo b_bias b_ohi b_olo b_y b_res b_tok b_copy b_stat b_var b_std b_sel b_scale b_vec b_feat
                   b_ft b_ftc b_l0 b_h1hi b_h1lo b_l1 b_h2hi b_h2lo b_l2 b_add b_back b_out b_store""".split()
        S = {n: sem(n) for n in names}
        nums = sorted(s.num for s in S.values())
        assert nums == list(range(nums[0], nums[0] + len(nums)))
        spent = range(nums[0], nums[-1] + 1)

        T = {
            "XH": sb("XH", [P, CT, HW], F32R),
            "XL": sb("XL", [P, CT, HW], F32R),
            "VS": sb("VS", [P, ST, HEADS, 2 * D], F32R),
            "QS": [sb(f"QS{i}", [P, HW], F32R) for i in range(2)],
            "KHL": [sb(f"KHL{i}", [P, 2, HW], F32R) for i in range(2)],
            "WQ": [sb(f"WQ{i}", [P, 2, CT, P], F32R) for i in range(2)],
            "OT": OT, "ident": ident, "b_qk": b_qk, "b_v": b_v, "bo_all": bo_all, "ramp": ramp, "iota": iota,
            "W0": W0, "W1H": W1H, "W1L": W1L, "W2S": W2S,
        }
        dram = {
            "x": x.rearrange("n (t p) s -> n p t s", p=P),
            "out": out.rearrange("n (t p) s -> n p t s", p=P),
            "wqk": wqk_s, "wv": wv_s, "wo": wo_s,
        }

        between(nc, "first", S, dram, T, None, 0)
        nc.all_engine_barrier(sems_to_clear=spent)
        with nc.Fori(0, N_IMG - 1) as img:
            attention(nc, "loop", S, dram, T)
            between(nc, "loop", S, dram, T, img, img + 1)
            nc.all_engine_barrier(sems_to_clear=spent)
        attention(nc, "last", S, dram, T)
        between(nc, "last", S, dram, T, N_IMG - 1, None)


def between(nc, tag, S, dram, T, done, nxt):
    with ExitStack() as c:
        X1 = None
        if done is not None:
            X1 = c.enter_context(nc.sbuf_tensor(f"X1_{tag}", [P, CT, HW], F32))
        norms(nc, tag, S, dram, T, X1, done, nxt)
        network(nc, tag, S, dram, T, X1, done, nxt)


def qk_project(pe, bank, W, XH, XL, chunk, part=(0, 12)):
    passes = [(w, xx, k) for w, xx in ((0, XH), (1, XH), (0, XL)) for k in range(CT)]
    for n in range(*part):
        w, xx, k = passes[n]
        mm = pe.matmul(bank, W[:, w, k, :], xx[:, k, chunk * 512:(chunk + 1) * 512],
                       start=(n == 0), stop=(n == len(passes) - 1))
    return mm


def rstd_of(dve, s_done, s_std, std, r, tmp, nb, mean, eps_var, base):
    n = base

    def step(ins):
        nonlocal n
        ins.then_inc(s_done, 1)
        n += 1
        dve.wait_ge(s_done, n)

    dve.wait_ge(s_std, 1)
    step(dve.reciprocal(r, std))
    step(dve.tensor_tensor(tmp, r, r, ALU.mult))
    step(dve.tensor_tensor(tmp, tmp, eps_var, ALU.mult))
    step(dve.tensor_scalar(tmp, tmp, -0.5, 1.5, ALU.mult, ALU.add))
    step(dve.tensor_tensor(r, r, tmp, ALU.mult))
    step(dve.scalar_tensor_tensor(out=nb, in0=mean, scalar=-1.0, in1=r, op0=ALU.mult, op1=ALU.mult))
    return n


def norms(nc, tag, S, dram, T, X1, done, nxt):
    back, front = done is not None, nxt is not None
    with ExitStack() as c:
        def sb(name, shape, dt=F32):
            return c.enter_context(nc.sbuf_tensor(f"{name}_{tag}", shape, dt))

        def bank(name):
            return c.enter_context(nc.psum_tensor(f"{name}_{tag}", [P, 512], F32))

        OT, XH, XL, ident = T["OT"], T["XH"], T["XL"], T["ident"]
        if back:
            OH = sb("OH", [P, CT, HW], F32R)
            OL = sb("OL", [P, CT, HW], F32R)
            WO = sb("WO", [P, 2, CT, C], F32R)
        if front:
            X = sb("X", [P, CT, HW])
            stats = sb("f_stats", [P, ST, 6])
            mv = sb("f_mv", [P, ST, 2])
            ev = sb("f_ev", [P, ST])
            std = sb("f_stdt", [P, ST])
            r = sb("f_r", [P, ST])
            tmp = sb("f_tmp", [P, ST])
            nb = sb("f_nb", [P, ST])
        pt = [bank(f"f_pt{i}") for i in range(3)]
        po = [bank(f"b_po{i}") for i in range(2)]
        block = c.enter_context(nc.Block())

        order = ["O0", "T0", "T1", "O1", "T2", "T3", "O2", "T4", "T5", "O3", "T6", "T7", "LN", "O4", "O5",
                 "B0", "B1", "O6", "B2", "B3", "O7", "B4", "B5", "B6", "B7"]
        order = [o for o in order if (back if o[0] == "O" else front)]

        def tile(s):
            return X[:, :, s * P:(s + 1) * P]

        @block.sync
        def _(sp):
            if back:
                for k in range(2):
                    sp.dma_start(f32(WO[:, k, :, :].rearrange("p k n -> p (k n)")), dram["wo"][:, k, :])\
                      .then_inc(S["b_wo"], 16)
                sp.dma_start(X1[:, 0, :], dram["x"][done, :, 0, :]).then_inc(S["b_x0"], 16)
            if front:
                for t in range(CT):
                    sp.dma_start(X[:, t, :], dram["x"][nxt, :, t, :]).then_inc(S["f_x"], 16)
            if back:
                for t in range(1, CT):
                    sp.dma_start(X1[:, t, :], dram["x"][done, :, t, :]).then_inc(S["b_x"], 16)
                sp.wait_ge(S["b_x"], 16 * (CT - 1))

        @block.tensor
        def _(pe):
            for o in order:
                n = int(o[1]) if o[1].isdigit() else 0
                if o[0] == "O":
                    t, half = divmod(n, NCH)
                    if n == 0:
                        pe.wait_ge(S["b_wo"], 32)
                        pe.wait_ge(S["b_olo"], CT)
                    if n >= 2:
                        pe.wait_ge(S["b_res"], n - 1)
                    passes = [(z, w, k) for z, w in ((OH, 0), (OL, 0), (OH, 1)) for k in range(CT)]
                    for m, (z, w, k) in enumerate(passes):
                        rows = z[:, k, t * 2 * P:(t + 1) * 2 * P].rearrange("p (c two) -> p c two", two=2)[:, :, half]
                        mm = pe.matmul(po[n % 2][:, :], rows, WO[:, w, k, :], start=(m == 0), stop=(m == 11))
                    mm.then_inc(S["b_y"], 1)
                elif o[0] == "T":
                    if n == 0:
                        pe.wait_ge(S["f_x"], 16 * CT)
                    if n >= 3:
                        pe.wait_ge(S["f_copy"], n - 2)
                    for t in range(CT):
                        mm = pe.transpose(pt[n % 3][:, t * P:(t + 1) * P], X[:, t, n * P:(n + 1) * P], ident[:, :])
                    mm.then_inc(S["f_tok"], 1)
                elif o[0] == "B":
                    pe.wait_ge(S["f_norm"], n + 1)
                    if n >= 3:
                        pe.wait_ge(S["f_lo"], n - 2)
                    for t in range(CT):
                        mm = pe.transpose(pt[n % 3][:, t * P:(t + 1) * P], X[:, t, n * P:(n + 1) * P], ident[:, :])
                    mm.then_inc(S["f_back"], 1)

        @block.scalar
        def _(act):
            if back:
                for k in range(CT):
                    act.activation(OH[:, k, :], OT[:, k, :], ACT.Copy).then_inc(S["b_ohi"], 1)
            for o in order:
                n = int(o[1]) if o[1].isdigit() else 0
                bank_tile = pt[n % 3][:, :].rearrange("p (t n) -> p t n", t=CT)
                if o[0] == "T":
                    act.wait_ge(S["f_tok"], n + 1)
                    act.activation(tile(n), bank_tile, ACT.Copy).then_inc(S["f_copy"], 1)
                elif o == "LN":
                    act.wait_ge(S["f_var"], 1)
                    act.activation(std[:, :], ev[:, :], ACT.Sqrt).then_inc(S["f_std"], 1)
                elif o[0] == "B":
                    act.wait_ge(S["f_back"], n + 1)
                    act.activation(XH[:, :, n * P:(n + 1) * P], bank_tile, ACT.Copy).then_inc(S["f_hi"], 1)

        @block.vector
        def _(dve):
            if back:
                for k in range(CT):
                    dve.wait_ge(S["b_ohi"], k + 1)
                    dve.tensor_tensor(OL[:, k, :], OT[:, k, :], f32(OH[:, k, :]), ALU.subtract)\
                       .then_inc(S["b_olo"], 1)
            for o in order:
                n = int(o[1]) if o[1].isdigit() else 0
                if o[0] == "O":
                    t, half = divmod(n, NCH)
                    xs = X1[:, t, half * 512:(half + 1) * 512]
                    dve.wait_ge(S["b_y"], n + 1)
                    dve.wait_ge(S["b_bias"], n + 1)
                    dve.tensor_tensor(xs, po[n % 2][:, :], xs, ALU.add).then_inc(S["b_res"], 1)
                elif o[0] == "T":
                    dve.wait_ge(S["f_copy"], n + 1)
                    dve.bn_stats(stats[:, n, :], tile(n)).then_inc(S["f_stat"], 1)
                elif o == "LN":
                    dve.wait_ge(S["f_stat"], ST)
                    for s in range(ST):
                        dve.bn_aggr(mv[:, s, :], stats[:, s, :]).then_inc(S["f_stat"], 1)
                    dve.wait_ge(S["f_stat"], 2 * ST)
                    dve.tensor_scalar(ev[:, :], mv[:, :, 1], 1e-6, None, ALU.add).then_inc(S["f_var"], 1)
                    rstd_of(dve, S["f_var"], S["f_std"], std[:, :], r[:, :], tmp[:, :], nb[:, :],
                            mv[:, :, 0], ev[:, :], 1)
                elif o[0] == "B":
                    dve.wait_ge(S["f_hi"], n + 1)
                    cs = slice(n * P, (n + 1) * P)
                    dve.tensor_tensor(XL[:, :, cs], pt[n % 3][:, :].rearrange("p (t n) -> p t n", t=CT),
                                      f32(XH[:, :, cs]), ALU.subtract).then_inc(S["f_lo"], 1)

        @block.gpsimd
        def _(pool):
            if back:
                for t in range(CT):
                    pool.wait_ge(S["b_x0" if t == 0 else "b_x"], 16 if t == 0 else 16 * (CT - 1))
                    for half in range(NCH):
                        xs = X1[:, t, half * 512:(half + 1) * 512]
                        pool.tensor_tensor(xs, xs, T["bo_all"][:, :], ALU.add).then_inc(S["b_bias"], 1)
            if front:
                pool.wait_ge(S["f_var"], 7)
                for s in range(ST):
                    pool.tensor_scalar(tile(s), tile(s), r[:, s:s + 1], nb[:, s:s + 1], ALU.mult, ALU.add)\
                        .then_inc(S["f_norm"], 1)


def network(nc, tag, S, dram, T, X1, done, nxt):
    back, front = done is not None, nxt is not None
    with ExitStack() as c:
        def sb(name, shape, dt=F32):
            return c.enter_context(nc.sbuf_tensor(f"{name}_{tag}", shape, dt))

        def bank(name):
            return c.enter_context(nc.psum_tensor(f"{name}_{tag}", [P, 512], F32))

        XH, XL, VS, QS, WQ = (T[k] for k in ("XH", "XL", "VS", "QS", "WQ"))
        KH, KL = ([z[:, i, :] for z in T["KHL"]] for i in range(2))
        ident, b_qk, W0, W1H, W1L, W2S = (T[k] for k in ("ident", "b_qk", "W0", "W1H", "W1L", "W2S"))
        if front:
            WV = sb("WV", [P, 2, CT, C], F32R)
        if back:
            XN = sb("XN", [P, ST, SEL])
            stats = sb("b_stats", [P, ST, 6])
            mv = sb("b_mv", [P, ST, 2])
            ev = sb("b_ev", [P, ST])
            std = sb("b_stdt", [P, ST])
            r = sb("b_r", [P, ST])
            r1 = sb("b_r1", [P, ST])
            tmp = sb("b_tmp", [P, ST])
            nb = sb("b_nb", [P, ST])
            above = sb("above", [P, ST, 64])
            idx = sb("idx", [P, ST, 2, 2])
            cmp3 = sb("cmp3", [P, ST, 3])
            mask = sb("mask", [P, ST, 2])
            mtmp = sb("mtmp", [P, ST, 2])
            active = sb("active", [P, ST])
            tmp16 = sb("tmp16", [P, 4 * ST])
            XNR = sb("XNR", [P, ST, 2], F32R)
            XNL = sb("XNL", [P, ST, 2])
            G = sb("G", [P, ST, 2, 5])
            F = sb("F", [P, ST, 2, NF])
            FT = sb("FT", [NF, 2 * HW], F32R)
            H1H = [sb(f"H1H{i}", [P, 3, 512], F32R) for i in range(2)]
            H1L = [sb(f"H1L{i}", [P, 3, 512], F32R) for i in range(2)]
            H2H = sb("H2H", [P, 2, 512], F32R)
            H2L = sb("H2L", [P, 2, 512], F32R)
            Y8 = sb("Y8", [P, 2 * ST, 8])
            Y4 = sb("Y4", [P, 2 * ST, 4])
            YS = sb("YS", [P, ST, 2, 2])
            YR = sb("YR", [P, ST, 2])
            EQ = sb("EQ", [P, ST, 2, 16])
            CY = sb("CY", [P, ST])
            ph = [bank(f"b_ph{i}") for i in range(3)]
            py = bank("b_py")
        pa = [bank(f"b_pa{i}") for i in range(2)]
        pv = [bank(f"f_pv{i}") for i in range(2)]
        NQ = 4
        block = c.enter_context(nc.Block())

        order = ["T0", "T1", "V0", "T2", "T3", "T4", "T5", "T6", "T7", "S0", "V1", "S1", "V2", "S2", "V3", "S3",
                 "V4", "F0", "F1", "F2", "F3", "L00", "V5", "L01", "L10", "V6", "L20", "L02", "L11", "V7", "L21",
                 "L03", "L12", "Q0", "L22", "Q1", "L13", "Q2", "L23", "S4", "Q3",
                 "R0", "R1", "R2", "R3", "R4", "R5", "R6", "R7"]
        order = [o for o in order if (front if o[0] in "VQ" else back)]

        def tile(s):
            return X1[:, :, s * P:(s + 1) * P]

        projected = [o for o in order if o[0] in "VQ"]

        @block.sync
        def _(sp):
            if front:
                for k in range(2):
                    sp.dma_start(f32(WV[:, k, :, :].rearrange("p k n -> p (k n)")), dram["wv"][:, k, :])\
                      .then_inc(S["f_wv"], 16)
                for h in range(2):
                    sp.dma_start(f32(WQ[h][:, :, :, :].rearrange("p a k n -> p a (k n)")), dram["wqk"][h])\
                      .then_inc(S[f"f_wqk{h}"], 16)
                for h in range(2):
                    sp.wait_ge(S["f_qk_lo"], NCH * (h + 1))
                    sp.dma_start(f32(KH[h][0:D, :]), f32(KH[h][D:P, :])).then_inc(S["f_kdup"], 16)
                    sp.dma_start(f32(KL[h][0:D, :]), f32(KL[h][D:P, :])).then_inc(S["f_kdup"], 16)
            if back:
                for n in range(NCH):
                    sp.wait_ge(S["b_out"], 4 * (n + 1))
                    cs = slice(n * 512, (n + 1) * 512)
                    sp.dma_start(dram["out"][done, :, :, cs], X1[:, :, cs]).then_inc(S["b_store"], 16)
                sp.wait_ge(S["b_store"], 16 * NCH)
            if front:
                sp.wait_ge(S["f_kdup"], 64)

        @block.gpsimd
        def _(pool):
            if back:
                pool.wait_ge(S["b_sel"], 1)
                for s in range(ST):
                    pool.tensor_scalar(tile(s), tile(s), r1[:, s:s + 1], nb[:, s:s + 1], ALU.mult, ALU.add)\
                        .then_inc(S["b_scale"], 1)

        @block.tensor
        def _(pe):
            for o in order:
                n = int(o[1:])
                if o[0] in "VQ":
                    i = projected.index(o)
                    if i >= 2:
                        if projected[i - 2][0] == "V":
                            pe.wait_ge(S["f_vlo"], i - 1)
                        else:
                            pe.wait_ge(S["f_qk_lo"], i - 1 - ST)
                    if o[0] == "V":
                        if n == 0:
                            pe.wait_ge(S["f_wv"], 32)
                        passes = [(z, w, k) for z, w in ((XH, 0), (XL, 0), (XH, 1)) for k in range(CT)]
                        for m, (z, w, k) in enumerate(passes):
                            mm = pe.matmul(pv[i % 2][:, :], z[:, k, n * P:(n + 1) * P], WV[:, w, k, :],
                                           start=(m == 0), stop=(m == len(passes) - 1))
                        mm.then_inc(S["f_v"], 1)
                    else:
                        h, chunk = divmod(n, NCH)
                        pe.wait_ge(S[f"f_wqk{h}"], 16)
                        qk_project(pe, pv[i % 2][:, :], WQ[h], XH, XL, chunk).then_inc(S["f_qk"], 1)
                elif o[0] == "T":
                    if n >= 2:
                        pe.wait_ge(S["b_copy"], n - 1)
                    for t in range(CT):
                        mm = pe.transpose(pa[n % 2][:, t * P:(t + 1) * P], X1[:, t, n * P:(n + 1) * P], ident[:, :])
                    mm.then_inc(S["b_tok"], 1)
                elif o[0] == "F":
                    if n == 0:
                        pe.wait_ge(S["b_feat"], 1)
                        pe.wait_ge(S["b_copy"], ST)
                    if n >= 2:
                        pe.wait_ge(S["b_ftc"], n - 1)
                    for k in range(4):
                        nib, s = divmod(4 * n + k, ST)
                        mm = pe.transpose(pa[n % 2][0:NF, k * P:(k + 1) * P], F[:, s, nib, :], ident[:, :])
                    mm.then_inc(S["b_ft"], 1)
                elif o[0:2] == "L0":
                    q = int(o[2])
                    pe.wait_ge(S["b_ftc"], q + 1)
                    for m in range(3):
                        if q >= 1:
                            pe.wait_ge(S["b_h1lo"], 3 * (q - 1) + m + 1)
                        pe.matmul(ph[m][:, :], W0[:, m, :], FT[:, q * 512:(q + 1) * 512], start=True, stop=True)\
                          .then_inc(S["b_l0"], 1)
                elif o[0:2] == "L1":
                    q = int(o[2])
                    if q == 0:
                        pe.wait_ge(S["b_ftc"], NQ)
                    for m in range(2):
                        if q >= 1:
                            pe.wait_ge(S["b_h2lo"], 2 * (q - 1) + m + 1)
                        i = 0
                        for k in range(3):
                            if m == 0:
                                pe.wait_ge(S["b_h1lo"], 3 * q + k + 1)
                            K = P if k < 2 else 2 * TAIL + 2
                            for w, hh in ((W1H, H1H), (W1L, H1H), (W1H, H1L)):
                                mm = pe.matmul(pa[m][:, :], w[0:K, k, m * P:(m + 1) * P], hh[q % 2][0:K, k, :],
                                               start=(i == 0), stop=(i == 8))
                                i += 1
                        mm.then_inc(S["b_l1"], 1)
                elif o[0:2] == "L2":
                    q = int(o[2])
                    pe.wait_ge(S["b_h2lo"], 2 * (q + 1))
                    for k in range(4):
                        j = 4 * q + k
                        ts = slice(k * P, (k + 1) * P)
                        for m in range(2):
                            K = P if m == 0 else TAIL + 2
                            pe.matmul(py[:, 8 * j:8 * j + 8], H2H[0:K, m, ts], W2S[0:K, m, :],
                                      start=(m == 0), stop=False)
                            mm = pe.matmul(py[:, 8 * j:8 * j + 8], H2L[0:K, m, ts], W2S[0:K, m, :],
                                           start=False, stop=(m == 1))
                    mm.then_inc(S["b_l2"], 1)
                elif o[0] == "R":
                    if n == 0:
                        pe.wait_ge(S["b_add"], 1)
                    if n >= 2:
                        pe.wait_ge(S["b_out"], n - 1)
                    for t in range(CT):
                        mm = pe.transpose(pa[n % 2][:, t * P:(t + 1) * P], X1[:, t, n * P:(n + 1) * P], ident[:, :])
                    mm.then_inc(S["b_back"], 1)

        @block.scalar
        def _(act):
            for o in order:
                n = int(o[1:])
                i = projected.index(o) if o in projected else 0
                if o[0] == "V":
                    act.wait_ge(S["f_v"], n + 1)
                    act.activation(VS[:, n, :, 0:D], pv[i % 2][:, :].rearrange("p (h d) -> p h d", h=HEADS),
                                   ACT.Copy).then_inc(S["f_vhi"], 1)
                elif o[0] == "Q":
                    h, chunk = divmod(n, NCH)
                    cs = slice(chunk * 512, (chunk + 1) * 512)
                    act.wait_ge(S["f_qk"], n + 1)
                    act.activation(QS[h][0:D, cs], pv[i % 2][0:D, :], ACT.Identity, bias=b_qk[0:D, h:h + 1])
                    act.activation(KH[h][D:P, cs], pv[i % 2][D:P, :], ACT.Identity, bias=b_qk[D:P, h:h + 1])\
                       .then_inc(S["f_qk_hi"], 1)
                elif o[0] == "T":
                    act.wait_ge(S["b_tok"], n + 1)
                    act.activation(tile(n), pa[n % 2][:, :].rearrange("p (t n) -> p t n", t=CT), ACT.Copy)\
                       .then_inc(S["b_copy"], 1)
                elif o == "S0":
                    act.wait_ge(S["b_var"], 1)
                    act.activation(std[:, :], ev[:, :], ACT.Sqrt).then_inc(S["b_std"], 1)
                elif o[0] == "F":
                    act.wait_ge(S["b_ft"], n + 1)
                    act.activation(FT[:, n * 512:(n + 1) * 512], pa[n % 2][0:NF, :], ACT.Copy)\
                       .then_inc(S["b_ftc"], 1)
                elif o[0:2] == "L0":
                    q = int(o[2])
                    for m in range(3):
                        act.wait_ge(S["b_l0"], 3 * q + m + 1)
                        if q >= 2 and m == 0:
                            act.wait_ge(S["b_l1"], 2 * (q - 1))
                        act.activation(H1H[q % 2][:, m, :], ph[m][:, :], ACT.Relu).then_inc(S["b_h1hi"], 1)
                elif o[0:2] == "L1":
                    q = int(o[2])
                    for m in range(2):
                        act.wait_ge(S["b_l1"], 2 * q + m + 1)
                        if q >= 1 and m == 0:
                            act.wait_ge(S["b_l2"], q)
                        act.activation(H2H[:, m, :], pa[m][:, :], ACT.Relu).then_inc(S["b_h2hi"], 1)
                elif o[0] == "R":
                    act.wait_ge(S["b_back"], n + 1)
                    act.activation(tile(n), pa[n % 2][:, :].rearrange("p (t n) -> p t n", t=CT), ACT.Copy)\
                       .then_inc(S["b_out"], 1)

        @block.vector
        def _(dve):
            count = [0]

            def step(ins):
                ins.then_inc(S["b_vec"], 1)
                count[0] += 1
                dve.wait_ge(S["b_vec"], count[0])

            def rstd():
                dve.wait_ge(S["b_stat"], ST)
                for s in range(ST):
                    dve.bn_aggr(mv[:, s, :], stats[:, s, :]).then_inc(S["b_stat"], 1)
                dve.wait_ge(S["b_stat"], 2 * ST)
                dve.tensor_scalar(ev[:, :], mv[:, :, 1], 1e-5, None, ALU.add).then_inc(S["b_var"], 1)
                dve.memset(F[:, :, :, :], 0.0)
                dve.memset(G[:, :, :, :], 1.0)
                rstd_of(dve, S["b_var"], S["b_std"], std[:, :], r[:, :], tmp[:, :], nb[:, :],
                        mv[:, :, 0], ev[:, :], 1)
                step(dve.tensor_scalar(r1[:, :], r[:, :], 1.0, None, ALU.add))

            def select():
                for s in range(ST):
                    last = dve.tensor_scalar(XN[:, s, :], X1[:, 0, s * P:s * P + SEL], r[:, s:s + 1], nb[:, s:s + 1],
                                             ALU.mult, ALU.add)
                last.then_inc(S["b_sel"], 1)
                dve.wait_ge(S["b_sel"], 1)

            def nibbles():
                group = above[:, :, :].rearrange("p s (g k) -> p (s g) k", k=16)
                step(dve.tensor_scalar(above[:, :, :], XN[:, :, 16:80], 0.5, None, ALU.is_gt))
                step(dve.tensor_tensor(group, group, T["ramp"][:, :].unsqueeze(1).to_broadcast([P, ST * 4, 16]),
                                       ALU.mult))
                flat = idx[:, :, :, :].rearrange("p s a b -> p (s a b)")
                step(dve.tensor_reduce(flat, group, AX.X, ALU.max))
                step(dve.tensor_scalar(tmp16[:, :], flat, -1.0, 16.0, ALU.mult, ALU.add))
                step(dve.scalar_tensor_tensor(out=flat, in0=flat, scalar=0.5, in1=tmp16[:, :],
                                              op0=ALU.is_gt, op1=ALU.mult))

            def features():
                step(dve.tensor_scalar(cmp3[:, :, :], XN[:, :, 0:3], 0.5, None, ALU.is_gt))
                dve.tensor_tensor(mask[:, :, 0], cmp3[:, :, 0], cmp3[:, :, 1], ALU.mult)
                dve.tensor_tensor(mtmp[:, :, 0], cmp3[:, :, 0], cmp3[:, :, 2], ALU.mult)
                dve.tensor_copy(XNR[:, :, :], XN[:, :, 105:107])
                step(dve.tensor_scalar(mtmp[:, :, 1], cmp3[:, :, 1], -1.0, 1.0, ALU.mult, ALU.add))
                step(dve.tensor_tensor(mask[:, :, 1], mtmp[:, :, 0], mtmp[:, :, 1], ALU.mult))
                dve.tensor_tensor(active[:, :], mask[:, :, 0], mask[:, :, 1], ALU.add)
                dve.tensor_tensor(XNL[:, :, :], XN[:, :, 105:107], f32(XNR[:, :, :]), ALU.subtract)
                for nib in range(2):
                    dve.tensor_copy(G[:, :, nib, 0:2], idx[:, :, :, nib])
                    last = dve.tensor_copy(G[:, :, nib, 2:4], f32(XNR[:, :, :]))
                step(last)
                for net in range(2):
                    mk = mask[:, :, net:net + 1]
                    for nib in range(2):
                        for base in (5 * net, 10 + 5 * net):
                            dve.tensor_tensor(F[:, :, nib, base:base + 5], G[:, :, nib, :],
                                              mk.to_broadcast([P, ST, 5]), ALU.mult)
                        for base in (20 + 2 * net, 24 + 2 * net):
                            last = dve.tensor_tensor(F[:, :, nib, base:base + 2], XNL[:, :, :],
                                                     mk.to_broadcast([P, ST, 2]), ALU.mult)
                last.then_inc(S["b_feat"], 1)

            def results():
                dve.wait_ge(S["b_l2"], NQ)
                step(dve.tensor_copy(Y8[:, :, :].rearrange("p j k -> p (j k)"), py[:, 0:16 * ST]))
                step(dve.tensor_tensor(Y4[:, :, :], Y8[:, :, 0:4], Y8[:, :, 4:8], ALU.add))
                for nib in range(2):
                    for v in range(2):
                        y = Y4[:, nib * ST:(nib + 1) * ST, 2 * v:2 * v + 2]
                        last = dve.tensor_tensor(y, y, mask[:, :, :], ALU.mult)
                step(last)
                for nib in range(2):
                    y = Y4[:, nib * ST:(nib + 1) * ST, :].rearrange("p s (v e) -> p s v e", e=2)
                    last = dve.tensor_tensor(YS[:, :, nib, :], y[:, :, :, 0], y[:, :, :, 1], ALU.add)
                step(last)
                step(dve.tensor_scalar(YR[:, :, :], YS[:, :, :, 0], -1.0, 16.0, ALU.max, ALU.min))
                step(dve.tensor_scalar(YR[:, :, :], YR[:, :, :], ROUND, None, ALU.add))
                step(dve.tensor_scalar(YR[:, :, :], YR[:, :, :], ROUND, None, ALU.subtract))
                step(dve.tensor_scalar(YR[:, :, :], YR[:, :, :], 0.0, 15.0, ALU.max, ALU.min))
                step(dve.scalar_tensor_tensor(out=YR[:, :, :], in0=YR[:, :, :], scalar=1.0,
                                              in1=active[:, :].unsqueeze(2).to_broadcast([P, ST, 2]),
                                              op0=ALU.add, op1=ALU.mult))
                step(dve.tensor_scalar(YR[:, :, :], YR[:, :, :], -1.0, None, ALU.add))
                dve.tensor_scalar(CY[:, :], YS[:, :, 1, 1], 0.5, None, ALU.is_gt)
                for nib in range(2):
                    last = dve.tensor_tensor(EQ[:, :, nib, :], T["iota"][:, :].unsqueeze(1).to_broadcast([P, ST, 16]),
                                             YR[:, :, nib:nib + 1].to_broadcast([P, ST, 16]), ALU.is_equal)
                step(last)
                dve.wait_ge(S["b_scale"], ST)
                wide = X1[:, 1, :].rearrange("p (s n) -> p s n", n=P)
                dve.scalar_tensor_tensor(out=wide[:, :, 0:32], in0=EQ[:, :, :, :].rearrange("p s n k -> p s (n k)"),
                                         scalar=2.0, in1=wide[:, :, 0:32], op0=ALU.mult, op1=ALU.add)
                dve.tensor_tensor(wide[:, :, 32], wide[:, :, 32], CY[:, :], ALU.add).then_inc(S["b_add"], 1)

            for o in order:
                n = int(o[1:])
                i = projected.index(o) if o in projected else 0
                if o[0] == "V":
                    dve.wait_ge(S["f_vhi"], n + 1)
                    dve.tensor_tensor(VS[:, n, :, D:2 * D], pv[i % 2][:, :].rearrange("p (h d) -> p h d", h=HEADS),
                                      f32(VS[:, n, :, 0:D]), ALU.subtract).then_inc(S["f_vlo"], 1)
                elif o[0] == "Q":
                    h, chunk = divmod(n, NCH)
                    dve.wait_ge(S["f_qk_hi"], n + 1)
                    split_qk(dve, pv[i % 2], QS[h], KH[h], KL[h], b_qk[:, h:h + 1], chunk)\
                        .then_inc(S["f_qk_lo"], 1)
                elif o[0] == "T":
                    dve.wait_ge(S["b_copy"], n + 1)
                    dve.bn_stats(stats[:, n, :], tile(n)).then_inc(S["b_stat"], 1)
                elif o == "S0":
                    rstd()
                elif o == "S1":
                    select()
                elif o == "S2":
                    nibbles()
                elif o == "S3":
                    features()
                elif o == "S4":
                    results()
                elif o[0:2] == "L0":
                    q = int(o[2])
                    for m in range(3):
                        dve.wait_ge(S["b_h1hi"], 3 * q + m + 1)
                        dve.scalar_tensor_tensor(out=H1L[q % 2][:, m, :], in0=ph[m][:, :], scalar=0.0,
                                                 in1=f32(H1H[q % 2][:, m, :]), op0=ALU.max, op1=ALU.subtract)\
                           .then_inc(S["b_h1lo"], 1)
                elif o[0:2] == "L1":
                    q = int(o[2])
                    for m in range(2):
                        dve.wait_ge(S["b_h2hi"], 2 * q + m + 1)
                        dve.scalar_tensor_tensor(out=H2L[:, m, :], in0=pa[m][:, :], scalar=0.0,
                                                 in1=f32(H2H[:, m, :]), op0=ALU.max, op1=ALU.subtract)\
                           .then_inc(S["b_h2lo"], 1)


def split_qk(dve, bank, QSb, KHb, KLb, bias, n):
    cs = slice(n * 512, (n + 1) * 512)
    dve.scalar_tensor_tensor(out=QSb[D:P, cs], in0=bank[0:D, :], scalar=bias[0:D, :], in1=f32(QSb[0:D, cs]),
                             op0=ALU.add, op1=ALU.subtract)
    return dve.scalar_tensor_tensor(out=KLb[D:P, cs], in0=bank[D:P, :], scalar=bias[D:P, :],
                                    in1=f32(KHb[D:P, cs]), op0=ALU.add, op1=ALU.subtract)


def attention(nc, tag, S, dram, T):
    with ExitStack() as c:
        def sb(name, shape, dt=F32):
            return c.enter_context(nc.sbuf_tensor(f"{name}_{tag}", shape, dt))

        XH, XL, VS, QS, WQ = (T[k] for k in ("XH", "XL", "VS", "QS", "WQ"))
        KH, KL = ([z[:, i, :] for z in T["KHL"]] for i in range(2))
        ident, b_qk, b_v, OT = (T[k] for k in ("ident", "b_qk", "b_v", "OT"))

        PR = [sb(f"PR{i}", [P, HW]) for i in range(2)]
        PH = [sb(f"PH{i}", [P, ST, 512], F32R) for i in range(2)]
        PL = [sb(f"PL{i}", [P, ST, 512], F32R) for i in range(2)]
        OB = [sb(f"OB{i}", [D, 512]) for i in range(2)]
        QK = sb("QK", [P, 512])
        HL = sb("HL", [P, 2, 512], F32R)
        nmax = sb("nmax", [P, STEPS])
        rsum = sb("rsum", [P, STEPS])
        rinv = sb("rinv", [P, STEPS])
        pS = [c.enter_context(nc.psum_tensor(f"pS{i}_{tag}", [P, HW], F32)) for i in range(2)]
        pT = [c.enter_context(nc.psum_tensor(f"pT{i}_{tag}", [P, 512], F32)) for i in range(2)]
        pJ = c.enter_context(nc.psum_tensor(f"pJ_{tag}", [P, 512], F32))
        pO = c.enter_context(nc.psum_tensor(f"pO_{tag}", [P, 512], F32))
        block = c.enter_context(nc.Block())

        def projection(g):
            head, r = (g + 6) // ST + 1, (g + 6) % ST
            return (head, r // 4, 3 * (r % 4), 3 * (r % 4) + 3) if 2 <= head < HEADS else None

        def splitting(g):
            head, r = (g + 2) // ST + 1, (g + 2) % ST
            return (head, r // 4) if r % 4 == 0 and 2 <= head < HEADS else None

        @block.sync
        def _(sp):
            def weights(h):
                sp.dma_start(f32(WQ[h % 2][:, :, :, :].rearrange("p a k n -> p a (k n)")), dram["wqk"][h])\
                  .then_inc(S[f"a_w{h % 2}"], 16)

            weights(2)
            weights(3)
            for h in range(2, HEADS):
                sp.wait_ge(S["a_scores"], ST * (h - 1))
                for n in range(NCH):
                    cs = slice(n * 512, (n + 1) * 512)
                    sp.wait_ge(S["a_proj_lo"], NCH * (h - 2) + n + 1)
                    for half in range(2):
                        ps = slice(half * D, (half + 1) * D)
                        sp.dma_start(f32(QS[h % 2][ps, cs]), f32(HL[0:D, half, :])).then_inc(S["a_qk"], 16)
                        sp.dma_start(f32(T["KHL"][h % 2][ps, :, cs]), f32(HL[D:P, :, :])).then_inc(S["a_qk"], 16)
                if h + 2 < HEADS:
                    weights(h + 2)
            sp.wait_ge(S["a_qk"], 64 * NCH * (HEADS - 2))

        @block.tensor
        def _(pe):
            def scores(g):
                h, t = divmod(g, ST)
                if t == 0 and h >= 2:
                    pe.wait_ge(S["a_qk"], 64 * NCH * (h - 1))
                if g >= 2:
                    pe.wait_ge(S["a_exp"], g - 1)
                q = QS[h % 2][:, t * P:(t + 1) * P]
                for n in range(NCH):
                    cs = slice(n * 512, (n + 1) * 512)
                    pe.matmul(pS[g % 2][:, cs], q, KH[h % 2][:, cs], start=True, stop=False)
                    mm = pe.matmul(pS[g % 2][:, cs], q, KL[h % 2][:, cs], start=False, stop=True)
                mm.then_inc(S["a_scores"], 1)

            def turn(g):
                pe.wait_ge(S["a_norm"], g + 1)
                for half in range(2):
                    if g >= 1:
                        pe.wait_ge(S["a_lo"], 2 * (g - 1) + half + 1)
                    for k in range(4):
                        kb = 4 * half + k
                        mm = pe.transpose(pT[half][:, k * P:(k + 1) * P], PR[g % 2][:, kb * P:(kb + 1) * P],
                                          ident[:, :])
                    mm.then_inc(S["a_tr"], 1)

            def project(h, chunk, *part):
                if part[0] == 0:
                    pe.wait_ge(S[f"a_w{h % 2}"], 16 * (h // 2))
                    if 2 * (h - 2) + chunk > 0:
                        pe.wait_ge(S["a_proj_out"], 2 * (h - 2) + chunk)
                mm = qk_project(pe, pJ[:, :], WQ[h % 2], XH, XL, chunk, part)
                if part[1] == 12:
                    mm.then_inc(S["a_proj"], 1)

            def values(ck, part):
                h = ck // 2
                if part == 0:
                    pe.wait_ge(S["a_lo"], 8 * (ck + 1))
                    if ck >= 1:
                        pe.wait_ge(S["a_o"], ck)
                for kb in (2 * part, 2 * part + 1):
                    v = VS[:, kb, h, :]
                    pe.matmul(pO[:, :], v, PH[ck % 2][:, kb, :], start=(kb == 0), stop=False)
                    mm = pe.matmul(pO[:, :], v, PL[ck % 2][:, kb, :], start=False, stop=(kb == ST - 1))
                if part == 3:
                    mm.then_inc(S["a_pv"], 1)

            scores(0)
            scores(1)
            for g in range(STEPS + 4):
                if g + 2 < STEPS:
                    scores(g + 2)
                if g >= 4 and g % 4 > 0:
                    values(g // 4 - 1, g % 4)
                if g < STEPS:
                    turn(g)
                if projection(g):
                    project(*projection(g))
                if g >= 4 and g % 4 == 0:
                    values(g // 4 - 1, 0)

        @block.scalar
        def _(act):
            def exp(g):
                act.wait_ge(S["a_max"], g + 1)
                if g >= 2:
                    act.wait_ge(S["a_tr"], 2 * (g - 1))
                act.activation(PR[g % 2][:, :], pS[g % 2][:, :], ACT.Exp, bias=nmax[:, g:g + 1],
                               accum_out=rsum[:, g:g + 1]).then_inc(S["a_exp"], 1)

            exp(0)
            for g in range(STEPS + 5):
                if g + 1 < STEPS:
                    exp(g + 1)
                if g >= 8 and g % 4 == 0:
                    ck = g // 4 - 2
                    act.wait_ge(S["a_pv"], ck + 1)
                    if ck >= 2:
                        act.wait_ge(S["a_o"], ck - 1)
                    act.activation(OB[ck % 2][:, :], pO[D:P, :], ACT.Identity,
                                   bias=b_v[D:P, ck // 2:ck // 2 + 1]).then_inc(S["a_obot"], 1)
                if splitting(g):
                    h, n = splitting(g)
                    i = NCH * (h - 2) + n
                    act.wait_ge(S["a_proj"], i + 1)
                    if i > 0:
                        act.wait_ge(S["a_proj_lo"], i)
                    act.activation(QK[:, :], pJ[:, :], ACT.Identity, bias=b_qk[:, h:h + 1])\
                       .then_inc(S["a_proj_out"], 1)
                if g < STEPS:
                    ck = g // 4
                    if ck >= 2:
                        act.wait_ge(S["a_pv"], ck - 1)
                    for half in range(2):
                        act.wait_ge(S["a_tr"], 2 * g + half + 1)
                        act.activation(PH[ck % 2][:, 4 * half:4 * half + 4, (g % 4) * P:(g % 4 + 1) * P],
                                       pT[half][:, :].rearrange("p (k n) -> p k n", k=4), ACT.Copy)\
                           .then_inc(S["a_hi"], 1)
                if splitting(g):
                    h, n = splitting(g)
                    i = NCH * (h - 2) + n
                    act.wait_ge(S["a_proj_out"], i + 1)
                    if i > 0:
                        act.wait_ge(S["a_qk"], 64 * i)
                    act.activation(HL[:, 0, :], QK[:, :], ACT.Copy).then_inc(S["a_proj_hi"], 1)

        @block.vector
        def _(dve):
            def rowmax(g):
                dve.wait_ge(S["a_scores"], g + 1)
                dve.tensor_reduce(nmax[:, g:g + 1], pS[g % 2][:, :], AX.X, ALU.max, negate=True)\
                   .then_inc(S["a_max"], 1)

            def recip(g):
                dve.wait_ge(S["a_exp"], g + 1)
                dve.reciprocal(rinv[:, g:g + 1], rsum[:, g:g + 1]).then_inc(S["a_recip"], 1)

            rowmax(0)
            rowmax(1)
            recip(0)
            for g in range(STEPS + 5):
                if g + 2 < STEPS:
                    rowmax(g + 2)
                if g + 1 < STEPS:
                    recip(g + 1)
                if g >= 8 and g % 4 == 0:
                    ck = g // 4 - 2
                    hh, n = divmod(ck, 2)
                    dve.wait_ge(S["a_obot"], ck + 1)
                    by_query = [z.rearrange("d (m jj jp) -> d jp jj m", jp=2, jj=CT) for z in (pO[0:D, :], OB[ck % 2][:, :])]
                    cols = slice(hh * P + n * D, hh * P + (n + 1) * D)
                    for jp in range(2):
                        last = dve.tensor_tensor(OT[jp * D:(jp + 1) * D, :, cols], by_query[0][:, jp], by_query[1][:, jp],
                                                 ALU.add)
                    last.then_inc(S["a_o"], 1)
                if g < STEPS:
                    ck = g // 4
                    for half in range(2):
                        ks = slice(4 * half, 4 * half + 4)
                        qs = slice((g % 4) * P, (g % 4 + 1) * P)
                        dve.wait_ge(S["a_hi"], 2 * g + half + 1)
                        dve.tensor_tensor(PL[ck % 2][:, ks, qs], pT[half][:, :].rearrange("p (k n) -> p k n", k=4),
                                          f32(PH[ck % 2][:, ks, qs]), ALU.subtract).then_inc(S["a_lo"], 1)

        @block.gpsimd
        def _(pool):
            for g in range(STEPS):
                pool.wait_ge(S["a_recip"], g + 1)
                pool.tensor_scalar(PR[g % 2][:, :], PR[g % 2][:, :], rinv[:, g:g + 1], 1.0, ALU.mult, ALU.mult)\
                    .then_inc(S["a_norm"], 1)
                if g >= 1 and splitting(g - 1):
                    h, n = splitting(g - 1)
                    i = NCH * (h - 2) + n
                    pool.wait_ge(S["a_proj_hi"], i + 1)
                    pool.tensor_tensor(HL[:, 1, :], QK[:, :], f32(HL[:, 0, :]), ALU.subtract)\
                        .then_inc(S["a_proj_lo"], 1)


def kernel(x, L0_conv_Wq, L0_conv_bq, L0_conv_Wk, L0_conv_bk, L0_conv_Wv, L0_conv_bv, L0_conv_Wo, L0_conv_bo,
           L0_ffn_Wa, L0_ffn_ba, L0_ffn_Ws, L0_ffn_bs):
    import numpy as np
    import concourse.bacc as bacc
    from concourse.bass_utils import run_bass_kernel_spmd

    f = np.float32
    x, wq, bq, wk, bk, wv, bv, wo, bo, wa, ba, ws, bs = [
        np.asarray(a) for a in (x, L0_conv_Wq, L0_conv_bq, L0_conv_Wk, L0_conv_bk, L0_conv_Wv, L0_conv_bv,
                                L0_conv_Wo, L0_conv_bo, L0_ffn_Wa, L0_ffn_ba, L0_ffn_Ws, L0_ffn_bs)]

    def by_channel(w):
        return w.T.reshape(CT, P, -1).transpose(1, 0, 2)

    q4, k4 = (by_channel(w).reshape(P, CT, HEADS, D).transpose(0, 2, 1, 3) for w in (wq, wk))
    wqk = np.concatenate([q4, k4], axis=3).reshape(P, -1)
    bqk = np.concatenate([bq.reshape(HEADS, D).T, bk.reshape(HEADS, D).T], axis=0)

    w0 = np.zeros((NF, 3, P), f)
    for net, (w, b) in enumerate(((wa, ba), (ws, bs))):
        cols = [w[0][:, i] for i in (0, 1, 35, 36)] + [b[0]]
        rows = [(5 * net + i, i) for i in range(5)] + [(10 + 5 * net + i, i) for i in range(5)]
        rows += [(20 + 2 * net + i, 2 + i) for i in range(2)] + [(24 + 2 * net + i, 2 + i) for i in range(2)]
        for row, i in rows:
            w0[row, net, :] = cols[i][0:P]
            w0[row, 2, net * TAIL:(net + 1) * TAIL] = cols[i][P:GE]
            if i == 4:
                w0[row, 2, 2 * TAIL + net] = 1.0
    takes_hi = np.array([1] * 10 + [0] * 10 + [1] * 4 + [0] * 8, f)
    w0mask = np.stack([takes_hi, 1 - takes_hi], axis=1)
    w1 = np.zeros((P, 3, 2, P), f)
    w2 = np.zeros((P, 2, 4), f)
    for net, (w, b) in enumerate(((wa, ba), (ws, bs))):
        wt = w[1].T
        for m, (o0, o1) in enumerate(((0, P), (P, GE))):
            w1[:, net, m, 0:o1 - o0] = wt[0:P, o0:o1]
            w1[net * TAIL:(net + 1) * TAIL, 2, m, 0:o1 - o0] = wt[P:GE, o0:o1]
            w1[2 * TAIL + net, 2, m, 0:o1 - o0] = b[1][o0:o1]
        w1[2 * TAIL + net, 2, 1, TAIL + net] = 1.0
        for v, o in enumerate((100, 101)):
            w2[:, 0, 2 * v + net] = w[2][o, 0:P]
            w2[0:TAIL, 1, 2 * v + net] = w[2][o, P:GE]
            w2[TAIL + net, 1, 2 * v + net] = b[2][o]

    arrays = {
        "x": x.reshape(N_IMG, C, HW),
        "wqk": wqk,
        "bqk": bqk,
        "wv": by_channel(wv).reshape(P, -1),
        "wo": by_channel(wo).reshape(P, -1),
        "bv": bv.reshape(HEADS, D).T,
        "bo_rep": np.repeat(bo[None, :], P, axis=0),
        "w0": w0.reshape(NF, -1),
        "w0mask": w0mask,
        "w1": w1.reshape(P, -1),
        "w2": w2,
        "ident": np.eye(P, dtype=f),
        "ramp": np.tile(np.arange(16, 0, -1, dtype=f)[None, :], (P, 1)),
        "iota": np.tile(np.arange(16, dtype=f)[None, :], (P, 1)),
    }
    arrays = {"in_" + k: np.ascontiguousarray(v) for k, v in arrays.items()}
    nc = bacc.Bacc("TRN2", target_bir_lowering=False, num_devices=1)
    aps = [nc.dram_tensor(k, v.shape, mybir.dt.from_np(v.dtype), kind="ExternalInput").ap()
           for k, v in arrays.items()]
    out = nc.dram_tensor("out_0", (N_IMG, C, HW), F32, kind="ExternalOutput").ap()
    build(nc, *aps, out)
    r = run_bass_kernel_spmd(nc, [arrays], core_ids=[0])
    return r.results[0]["out_0"].reshape(N_IMG, C, 32, 32)
```

```python
from contextlib import ExitStack

import concourse.bass as bass
from concourse import mybir

ALU = mybir.AluOpType
ACT = mybir.ActivationFunctionType
AX = mybir.AxisListType
F32 = mybir.dt.float32
F32R = mybir.dt.float32r

P = 128
N_IMG, C, HW = 8, 512, 1024
HEADS = 8
D = C // HEADS
CT = C // P
ST = HW // P
NCH = HW // 512
STEPS = HEADS * ST
GE = 160
TAIL = GE - P
SEL = 112
NF = 32
ROUND = 12582912.0
QSCALE = 1.0 / 8.0


def f32(ap):
    return ap.bitcast(F32)


def build(nc, x, wqk, bqk, wv, wo, bv, bo_rep, w0, w0mask, w1, w2, ident_d, ramp_d, iota_d, out):
    ctx = ExitStack()
    with ctx:
        def sb(name, shape, dt=F32, c=ctx):
            return c.enter_context(nc.sbuf_tensor(name, shape, dt))

        def ps(name, shape, c, dt=F32):
            return c.enter_context(nc.psum_tensor(name, shape, dt))

        def sem(name):
            return ctx.enter_context(nc.semaphore(name))

        wqk_s = nc.dram_tensor("wqk_split", (HEADS, P, 2, CT * P), F32, kind="Internal").ap()
        wv_s = nc.dram_tensor("wv_split", (P, 2, CT * C), F32, kind="Internal").ap()
        wo_s = nc.dram_tensor("wo_split", (P, 2, CT * C), F32, kind="Internal").ap()

        ident = sb("ident", [P, P])
        b_qk = sb("b_qk", [P, HEADS])
        b_v = sb("b_v", [P, HEADS])
        bo_all = sb("bo_all", [P, C])
        ramp = sb("ramp", [P, 16])
        iota = sb("iota", [P, 16])
        W0 = sb("W0", [NF, 3, P], F32R)
        W1H = sb("W1H", [P, 3, 2 * P], F32R)
        W1L = sb("W1L", [P, 3, 2 * P], F32R)
        W2S = sb("W2S", [P, 2, P], F32R)
        OT = sb("OT", [P, CT, HW])

        names = """f_x b_wo f_wv f_wqk0 f_wqk1 f_tok f_copy f_stat f_var f_std f_norm f_back f_hi f_lo f_v f_vhi f_vlo
                   f_qk f_qk_hi f_qk_lo f_kdup0 f_kdup1
                   a_w0 a_w1 a_scores a_max a_exp a_recip a_norm a_tr a_hi a_lo a_pv a_obot a_o a_proj a_proj_out a_proj_hi
                   a_proj_lo a_qk
                   b_x0 b_x1 b_x2 b_x3 b_bias b_ohi b_olo b_y b_res b_tok b_copy b_stat b_var b_std b_sel b_scale b_vec b_feat
                   b_ft b_ftc b_l0 b_h1hi b_h1lo b_l1 b_h2hi b_h2lo b_l2 b_yf b_yt b_add b_back b_out b_store""".split()
        S = {n: sem(n) for n in names}
        nums = sorted(s.num for s in S.values())
        assert nums == list(range(nums[0], nums[0] + len(nums)))
        loaded = range(nums[0], nums[0] + 2)
        spent = range(nums[0] + 2, nums[-1] + 1)
        assert {S["f_x"].num, S["b_wo"].num} == set(loaded)

        at_XH = nc.sbuf_base
        XH = sb("XH", [P, CT, HW], F32R)
        WO = nc.alloc_sbuf_tensor_at("WO", [P, 2, CT, C], F32R, offset=at_XH)
        at_XL = nc.sbuf_base
        XL = sb("XL", [P, CT, HW], F32R)
        X = nc.alloc_sbuf_tensor_at("X", [P, CT, HW], F32, offset=at_XL)
        assert at_XH % 32 == 0 and at_XL - at_XH == CT * HW * 4
        T = {
            "XH": XH, "XL": XL, "WO": WO, "X": X,
            "VS": sb("VS", [P, ST, HEADS, 2 * D], F32R),
            "QS": [sb(f"QS{i}", [P, HW], F32R) for i in range(2)],
            "KHL": [sb(f"KHL{i}", [P, 2, HW], F32R) for i in range(2)],
            "WQ": [sb(f"WQ{i}", [P, 2, CT, P], F32R) for i in range(2)],
            "OT": OT, "ident": ident, "b_qk": b_qk, "b_v": b_v, "bo_all": bo_all, "ramp": ramp, "iota": iota,
            "W0": W0, "W1H": W1H, "W1L": W1L, "W2S": W2S,
        }
        T["WV"] = [z[:, :, :].rearrange("p a (b n) -> p (a b) n", n=C) for z in T["KHL"]]
        dram = {
            "x": x.rearrange("n (t p) s -> n p t s", p=P),
            "out": out.rearrange("n (t p) s -> n p t s", p=P),
            "wqk": wqk_s, "wv": wv_s, "wo": wo_s,
        }

        s_ident_in, s_v_in, s_o_in, s_qk_in, s_small_in = (
            sem("s_" + n) for n in ("ident_in", "wv_in", "wo_in", "wqk_in", "small_in"))
        s_scaled = sem("s_scaled")
        s_w_hi = sem("s_w_hi")
        s_w_lo = sem("s_w_lo")
        s_small = sem("s_small")
        for n in ("wv_out", "wo_out", "wqk_out"):
            S[n] = sem("s_" + n)
        with ExitStack() as pc:
            raw = sb("raw", [P, HEADS * CT * P], F32, pc)
            hi = sb("hi", [P, HEADS * CT * P], F32R, pc)
            lo = sb("lo", [P, HEADS * CT * P], F32R, pc)
            rawv = sb("rawv", [P, CT, C], F32, pc)
            rawo = sb("rawo", [P, CT, C], F32, pc)
            w0r = sb("w0r", [NF, 3 * P], F32, pc)
            w0h = sb("w0h", [NF, 3 * P], F32R, pc)
            w0l = sb("w0l", [NF, 3 * P], F32, pc)
            w0m = sb("w0m", [NF, 2], F32, pc)
            w1r = sb("w1r", [P, 3 * 2 * P], F32, pc)
            w2r = sb("w2r", [P, 2, P - 4], F32, pc)
            small = [(b_v[D:P, :], bv), (bo_all[:, :], bo_rep), (b_qk[:, :], bqk), (ramp[:, :], ramp_d),
                     (iota[:, :], iota_d), (w0r[:, :], w0), (w0m[:, :], w0mask), (w1r[:, :], w1),
                     (w2r[:, :, :], w2)]
            raw_q = raw[:, :].rearrange("p (a b) -> p a b", b=P)[:, :, 0:D]
            WV = T["WV"]
            with nc.Block() as block:
                @block.sync
                def _(sp):
                    sp.dma_start(rawv[:, :, :].rearrange("p k n -> p (k n)"), wv).then_inc(s_v_in, 16)
                    sp.dma_start(ident[:, :], ident_d).then_inc(s_ident_in, 16)
                    for t in range(CT):
                        sp.dma_start(X[:, t, :], dram["x"][0, :, t, :]).then_inc(S["f_x"], 16)
                    sp.dma_start(raw[:, :], wqk).then_inc(s_qk_in, 16)
                    sp.dma_start(rawo[:, :, :].rearrange("p k n -> p (k n)"), wo).then_inc(s_o_in, 16)
                    for dst, src in small:
                        sp.dma_start(dst, src).then_inc(s_small_in, 16)
                    sp.wait_ge(s_w_lo, 1)
                    for k in range(2):
                        sp.dma_start(wv_s[:, k, :], f32(WV[k].rearrange("p k n -> p (k n)"))).then_inc(S["wv_out"], 16)
                    sp.wait_ge(s_w_lo, 2)
                    for k, half in enumerate((hi, lo)):
                        sp.dma_start(wqk_s[:, :, k, :].rearrange("h p n -> p h n"),
                                     f32(half[:, :].rearrange("p (h n) -> p h n", h=HEADS))).then_inc(S["wqk_out"], 16)
                    sp.wait_ge(s_w_lo, 3)
                    for k in range(2):
                        sp.dma_start(wo_s[:, k, :], f32(WO[:, k, :, :].rearrange("p k n -> p (k n)")))\
                          .then_inc(S["wo_out"], 16)
                    sp.wait_ge(s_ident_in, 16)

                @block.scalar
                def _(act):
                    act.wait_ge(s_v_in, 16)
                    act.activation(WV[0], rawv[:, :, :], ACT.Copy).then_inc(s_w_hi, 1)
                    act.wait_ge(s_scaled, 1)
                    act.activation(hi[:, :], raw[:, :], ACT.Copy).then_inc(s_w_hi, 1)
                    act.wait_ge(s_o_in, 16)
                    act.activation(WO[:, 0, :, :], rawo[:, :, :], ACT.Copy).then_inc(s_w_hi, 1)
                    act.wait_ge(s_small_in, 16 * len(small))
                    act.activation(w0h[:, :], w0r[:, :], ACT.Copy).then_inc(s_w_hi, 1)
                    act.activation(W1H[:, :, :].rearrange("p a b -> p (a b)"), w1r[:, :], ACT.Copy)\
                       .then_inc(s_w_hi, 1)
                    act.activation(W2S[:, :, 0:4], w2r[:, :, 0:4], ACT.Copy).then_inc(s_w_hi, 1)

                @block.vector
                def _(dve):
                    dve.wait_ge(s_w_hi, 1)
                    dve.tensor_tensor(WV[1], rawv[:, :, :], f32(WV[0]), ALU.subtract).then_inc(s_w_lo, 1)
                    dve.wait_ge(s_qk_in, 16)
                    dve.tensor_scalar(raw_q, raw_q, QSCALE, None, ALU.mult).then_inc(s_scaled, 1)
                    dve.wait_ge(s_scaled, 1)
                    dve.wait_ge(s_w_hi, 2)
                    dve.tensor_tensor(lo[:, :], raw[:, :], f32(hi[:, :]), ALU.subtract).then_inc(s_w_lo, 1)
                    dve.wait_ge(s_w_hi, 3)
                    dve.tensor_tensor(WO[:, 1, :, :], rawo[:, :, :], f32(WO[:, 0, :, :]), ALU.subtract)\
                       .then_inc(s_w_lo, 1)
                    dve.wait_ge(s_small_in, 16 * len(small))
                    dve.tensor_scalar(b_qk[0:D, :], b_qk[0:D, :], QSCALE, None, ALU.mult)
                    dve.wait_ge(s_w_hi, 6)
                    dve.tensor_tensor(w0l[:, :], w0r[:, :], f32(w0h[:, :]), ALU.subtract).then_inc(s_small, 1)
                    dve.tensor_tensor(W1L[:, :, :].rearrange("p a b -> p (a b)"), w1r[:, :],
                                      f32(W1H[:, :, :].rearrange("p a b -> p (a b)")), ALU.subtract)
                    dve.tensor_tensor(W2S[:, :, 4:8], w2r[:, :, 0:4], f32(W2S[:, :, 0:4]), ALU.subtract)
                    dve.tensor_copy(W2S[:, :, 8:P], w2r[:, :, 4:P - 4])
                    dve.wait_ge(s_small, 1)
                    dve.tensor_scalar(w0l[:, :], w0l[:, :], w0m[:, 1:2], None, ALU.mult).then_inc(s_small, 1)
                    dve.wait_ge(s_small, 2)
                    dve.scalar_tensor_tensor(out=W0[:, :, :].rearrange("p a b -> p (a b)"), in0=f32(w0h[:, :]),
                                             scalar=w0m[:, 0:1], in1=w0l[:, :], op0=ALU.mult, op1=ALU.add)

            between(nc, "first", S, dram, T, None, 0)
        nc.all_engine_barrier(sems_to_clear=loaded)
        with nc.Fori(0, N_IMG - 1) as img:
            attention(nc, "loop", S, dram, T, img + 1)
            nc.all_engine_barrier(sems_to_clear=spent)
            between(nc, "loop", S, dram, T, img, img + 1)
            nc.all_engine_barrier(sems_to_clear=loaded)
        attention(nc, "last", S, dram, T, None)
        nc.all_engine_barrier(sems_to_clear=spent)
        between(nc, "last", S, dram, T, N_IMG - 1, None)


def between(nc, tag, S, dram, T, done, nxt):
    with ExitStack() as c:
        X1 = None
        if done is not None:
            X1 = c.enter_context(nc.sbuf_tensor(f"X1_{tag}", [P, CT, HW], F32))
        norms(nc, tag, S, dram, T, X1, done, nxt)
        network(nc, tag, S, dram, T, X1, done, nxt)


def qk_project(pe, bank, W, XH, XL, chunk, part=(0, 12)):
    passes = [(w, xx, k) for w, xx in ((0, XH), (1, XH), (0, XL)) for k in range(CT)]
    for n in range(*part):
        w, xx, k = passes[n]
        mm = pe.matmul(bank, W[:, w, k, :], xx[:, k, chunk * 512:(chunk + 1) * 512],
                       start=(n == 0), stop=(n == len(passes) - 1))
    return mm


def rstd_of(dve, s_done, s_std, std, r, tmp, nb, mean, eps_var, base):
    n = base

    def step(ins):
        nonlocal n
        ins.then_inc(s_done, 1)
        n += 1
        dve.wait_ge(s_done, n)

    dve.wait_ge(s_std, 1)
    step(dve.reciprocal(r, std))
    step(dve.tensor_tensor(tmp, r, r, ALU.mult))
    step(dve.tensor_tensor(tmp, tmp, eps_var, ALU.mult))
    step(dve.tensor_scalar(tmp, tmp, -0.5, 1.5, ALU.mult, ALU.add))
    step(dve.tensor_tensor(r, r, tmp, ALU.mult))
    step(dve.scalar_tensor_tensor(out=nb, in0=mean, scalar=-1.0, in1=r, op0=ALU.mult, op1=ALU.mult))
    return n


def norms(nc, tag, S, dram, T, X1, done, nxt):
    back, front = done is not None, nxt is not None
    with ExitStack() as c:
        def sb(name, shape, dt=F32):
            return c.enter_context(nc.sbuf_tensor(f"{name}_{tag}", shape, dt))

        def bank(name):
            return c.enter_context(nc.psum_tensor(f"{name}_{tag}", [P, 512], F32))

        OT, XH, XL, WO, X, ident = (T[k] for k in ("OT", "XH", "XL", "WO", "X", "ident"))
        if back:
            OH = sb("OH", [P, CT, HW], F32R)
            OL = sb("OL", [P, CT, HW], F32R)
        if front:
            stats = sb("f_stats", [P, ST, 6])
            mv = sb("f_mv", [P, ST, 2])
            ev = sb("f_ev", [P, ST])
            std = sb("f_stdt", [P, ST])
            r = sb("f_r", [P, ST])
            tmp = sb("f_tmp", [P, ST])
            nb = sb("f_nb", [P, ST])
        pt = [bank(f"f_pt{i}") for i in range(3)]
        po = [bank(f"b_po{i}") for i in range(2)]
        block = c.enter_context(nc.Block())

        order = ["H0", "T0", "T1", "T2", "O0", "H1", "T3", "O1", "T4", "T5", "O2", "H2", "T6", "T7", "O3", "LN",
                 "O4", "H3", "O5", "O6", "O7", "B0", "B1", "B2", "B3", "B4", "B5", "B6", "B7"]
        order = [o for o in order if (back if o[0] in "HO" else front)]

        def tile(s):
            return X[:, :, s * P:(s + 1) * P]

        @block.sync
        def _(sp):
            if back:
                for t in range(CT):
                    sp.dma_start(X1[:, t, :], dram["x"][done, :, t, :]).then_inc(S[f"b_x{t}"], 16)
            if front and back:
                for k in range(2):
                    sp.dma_start(f32(T["WV"][k].rearrange("p k n -> p (k n)")), dram["wv"][:, k, :])\
                      .then_inc(S["f_wv"], 16)
            if front:
                if not back:
                    sp.wait_ge(S["wqk_out"], 32)
                for h in range(2):
                    sp.dma_start(f32(T["WQ"][h][:, :, :, :].rearrange("p a k n -> p a (k n)")), dram["wqk"][h])\
                      .then_inc(S[f"f_wqk{h}"], 16)

        @block.tensor
        def _(pe):
            for o in order:
                n = int(o[1]) if o[1].isdigit() else 0
                if o[0] == "O":
                    t, half = divmod(n, NCH)
                    if n == 0:
                        pe.wait_ge(S["b_wo"], 32)
                    if half == 0:
                        pe.wait_ge(S["b_olo"], t + 1)
                    if n >= 2:
                        pe.wait_ge(S["b_res"], n - 1)
                    passes = [(z, w, k) for z, w in ((OH, 0), (OL, 0), (OH, 1)) for k in range(CT)]
                    for m, (z, w, k) in enumerate(passes):
                        rows = z[:, k, t * 2 * P:(t + 1) * 2 * P].rearrange("p (c two) -> p c two", two=2)[:, :, half]
                        mm = pe.matmul(po[n % 2][:, :], rows, WO[:, w, k, :], start=(m == 0), stop=(m == 11))
                    mm.then_inc(S["b_y"], 1)
                elif o[0] == "T":
                    if n == 0:
                        pe.wait_ge(S["f_x"], 16 * CT)
                    if n >= 3:
                        pe.wait_ge(S["f_copy"], n - 2)
                    for t in range(CT):
                        mm = pe.transpose(pt[n % 3][:, t * P:(t + 1) * P], X[:, t, n * P:(n + 1) * P], ident[:, :])
                    mm.then_inc(S["f_tok"], 1)
                elif o[0] == "B":
                    pe.wait_ge(S["f_norm"], n + 1)
                    if n >= 3:
                        pe.wait_ge(S["f_lo"], n - 2)
                    for t in range(CT):
                        mm = pe.transpose(pt[n % 3][:, t * P:(t + 1) * P], X[:, t, n * P:(n + 1) * P], ident[:, :])
                    mm.then_inc(S["f_back"], 1)

        @block.scalar
        def _(act):
            for o in order:
                n = int(o[1]) if o[1].isdigit() else 0
                bank_tile = pt[n % 3][:, :].rearrange("p (t n) -> p t n", t=CT)
                if o[0] == "H":
                    rows = slice(n * 2 * P, (n + 1) * 2 * P)
                    act.activation(OH[:, :, rows], OT[:, :, rows], ACT.Copy).then_inc(S["b_ohi"], 1)
                elif o[0] == "T":
                    act.wait_ge(S["f_tok"], n + 1)
                    act.activation(tile(n), bank_tile, ACT.Copy).then_inc(S["f_copy"], 1)
                elif o == "LN":
                    act.wait_ge(S["f_var"], 1)
                    act.activation(std[:, :], ev[:, :], ACT.Sqrt).then_inc(S["f_std"], 1)
                elif o[0] == "B":
                    if n == 0 and not back:
                        act.wait_ge(S["wo_out"], 32)
                    act.wait_ge(S["f_back"], n + 1)
                    act.activation(XH[:, :, n * P:(n + 1) * P], bank_tile, ACT.Copy).then_inc(S["f_hi"], 1)

        @block.vector
        def _(dve):
            for o in order:
                n = int(o[1]) if o[1].isdigit() else 0
                if o[0] == "H":
                    rows = slice(n * 2 * P, (n + 1) * 2 * P)
                    dve.wait_ge(S["b_ohi"], n + 1)
                    dve.tensor_tensor(OL[:, :, rows], OT[:, :, rows], f32(OH[:, :, rows]), ALU.subtract)\
                       .then_inc(S["b_olo"], 1)
                elif o[0] == "O":
                    t, half = divmod(n, NCH)
                    xs = X1[:, t, half * 512:(half + 1) * 512]
                    dve.wait_ge(S["b_y"], n + 1)
                    dve.wait_ge(S["b_bias"], n + 1)
                    dve.tensor_tensor(xs, po[n % 2][:, :], xs, ALU.add).then_inc(S["b_res"], 1)
                elif o[0] == "T":
                    dve.wait_ge(S["f_copy"], n + 1)
                    dve.bn_stats(stats[:, n, :], tile(n)).then_inc(S["f_stat"], 1)
                elif o == "LN":
                    dve.wait_ge(S["f_stat"], ST)
                    for s in range(ST):
                        dve.bn_aggr(mv[:, s, :], stats[:, s, :]).then_inc(S["f_stat"], 1)
                    dve.wait_ge(S["f_stat"], 2 * ST)
                    dve.tensor_scalar(ev[:, :], mv[:, :, 1], 1e-6, None, ALU.add).then_inc(S["f_var"], 1)
                    rstd_of(dve, S["f_var"], S["f_std"], std[:, :], r[:, :], tmp[:, :], nb[:, :],
                            mv[:, :, 0], ev[:, :], 1)
                elif o[0] == "B":
                    dve.wait_ge(S["f_hi"], n + 1)
                    cs = slice(n * P, (n + 1) * P)
                    dve.tensor_tensor(XL[:, :, cs], pt[n % 3][:, :].rearrange("p (t n) -> p t n", t=CT),
                                      f32(XH[:, :, cs]), ALU.subtract).then_inc(S["f_lo"], 1)

        @block.gpsimd
        def _(pool):
            if back:
                for t in range(CT):
                    pool.wait_ge(S[f"b_x{t}"], 16)
                    for half in range(NCH):
                        xs = X1[:, t, half * 512:(half + 1) * 512]
                        pool.tensor_tensor(xs, xs, T["bo_all"][:, :], ALU.add).then_inc(S["b_bias"], 1)
            if front:
                pool.wait_ge(S["f_var"], 7)
                for s in range(ST):
                    pool.tensor_scalar(tile(s), tile(s), r[:, s:s + 1], nb[:, s:s + 1], ALU.mult, ALU.add)\
                        .then_inc(S["f_norm"], 1)


def network(nc, tag, S, dram, T, X1, done, nxt):
    back, front = done is not None, nxt is not None
    with ExitStack() as c:
        def sb(name, shape, dt=F32):
            return c.enter_context(nc.sbuf_tensor(f"{name}_{tag}", shape, dt))

        def bank(name):
            return c.enter_context(nc.psum_tensor(f"{name}_{tag}", [P, 512], F32))

        XH, XL, VS, QS, WQ = (T[k] for k in ("XH", "XL", "VS", "QS", "WQ"))
        KH, KL = ([z[:, i, :] for z in T["KHL"]] for i in range(2))
        ident, b_qk, W0, W1H, W1L, W2S = (T[k] for k in ("ident", "b_qk", "W0", "W1H", "W1L", "W2S"))
        WV = T["WV"]
        if back:
            XN = sb("XN", [P, ST, SEL])
            stats = sb("b_stats", [P, ST, 6])
            mv = sb("b_mv", [P, ST, 2])
            ev = sb("b_ev", [P, ST])
            std = sb("b_stdt", [P, ST])
            r = sb("b_r", [P, ST])
            r1 = sb("b_r1", [P, ST])
            tmp = sb("b_tmp", [P, ST])
            nb = sb("b_nb", [P, ST])
            above = sb("above", [P, ST, 64])
            idx = sb("idx", [P, ST, 2, 2])
            cmp3 = sb("cmp3", [P, ST, 3])
            mask = sb("mask", [P, ST, 2])
            mtmp = sb("mtmp", [P, ST, 2])
            active = sb("active", [P, ST])
            tmp16 = sb("tmp16", [P, 4 * ST])
            XNR = sb("XNR", [P, ST, 2], F32R)
            XNL = sb("XNL", [P, ST, 2])
            G = sb("G", [P, ST, 2, 5])
            F = sb("F", [P, ST, 2, NF])
            FT = sb("FT", [NF, 2 * HW], F32R)
            H1H = [sb(f"H1H{i}", [P, 3, 512], F32R) for i in range(2)]
            H1L = [sb(f"H1L{i}", [P, 3, 512], F32R) for i in range(2)]
            H2H = sb("H2H", [P, 2, 512], F32R)
            H2L = sb("H2L", [P, 2, 512], F32R)
            YF = sb("YF", [8, 2 * HW])
            Y8 = sb("Y8", [P, 2 * ST, 8])
            Y4 = sb("Y4", [P, 2 * ST, 4])
            YS = sb("YS", [P, ST, 2, 2])
            YR = sb("YR", [P, ST, 2])
            EQ = sb("EQ", [P, ST, 2, 16])
            CY = sb("CY", [P, ST])
            ph = [bank(f"b_ph{i}") for i in range(3)]
            py = bank("b_py")
        pa = [bank(f"b_pa{i}") for i in range(2)]
        pv = [bank(f"f_pv{i}") for i in range(2)]
        NQ = 4
        block = c.enter_context(nc.Block())

        order = ["T0", "T1", "T2", "T3", "V0", "T4", "T5", "T6", "T7", "S0", "V1", "S1", "V2", "S2", "V3", "S3",
                 "V4", "V5", "F0", "F1", "F2", "F3", "L00", "L01", "L10", "V6", "L20", "L02", "L11", "V7", "L21",
                 "L03", "L12", "Q0", "L22", "Q1", "L13", "Q2", "L23", "Y0", "S4", "Q3",
                 "R0", "R1", "R2", "R3", "R4", "R5", "R6", "R7"]
        order = [o for o in order if (front if o[0] in "VQ" else back)]

        def tile(s):
            return X1[:, :, s * P:(s + 1) * P]

        projected = [o for o in order if o[0] in "VQ"]

        @block.sync
        def _(sp):
            if front:
                for h in range(2):
                    sp.wait_ge(S["f_qk_lo"], NCH * (h + 1))
                    sp.dma_start(f32(T["KHL"][h][0:D, :, :]), f32(T["KHL"][h][D:P, :, :]))\
                      .then_inc(S[f"f_kdup{h}"], 16)
                    sp.dma_start(f32(WQ[h][:, :, :, :].rearrange("p a k n -> p a (k n)")), dram["wqk"][h + 2])\
                      .then_inc(S[f"a_w{h}"], 16)
            if back:
                for n in range(NCH):
                    sp.wait_ge(S["b_out"], 4 * (n + 1))
                    cs = slice(n * 512, (n + 1) * 512)
                    sp.dma_start(dram["out"][done, :, :, cs], X1[:, :, cs]).then_inc(S["b_store"], 16)
                if not front:
                    sp.wait_ge(S["b_store"], 16 * NCH)

        @block.gpsimd
        def _(pool):
            if back:
                pool.wait_ge(S["b_sel"], 1)
                for s in range(ST):
                    pool.tensor_scalar(tile(s), tile(s), r1[:, s:s + 1], nb[:, s:s + 1], ALU.mult, ALU.add)\
                        .then_inc(S["b_scale"], 1)

        @block.tensor
        def _(pe):
            for o in order:
                n = int(o[1:])
                if o[0] in "VQ":
                    i = projected.index(o)
                    if i >= 2:
                        if projected[i - 2][0] == "V":
                            pe.wait_ge(S["f_vlo"], i - 1)
                        else:
                            pe.wait_ge(S["f_qk_lo"], i - 1 - ST)
                    if o[0] == "V":
                        if n == 0 and back:
                            pe.wait_ge(S["f_wv"], 32)
                        passes = [(z, w, k) for z, w in ((XH, 0), (XL, 0), (XH, 1)) for k in range(CT)]
                        for m, (z, w, k) in enumerate(passes):
                            mm = pe.matmul(pv[i % 2][:, :], z[:, k, n * P:(n + 1) * P], WV[w][:, k, :],
                                           start=(m == 0), stop=(m == len(passes) - 1))
                        mm.then_inc(S["f_v"], 1)
                    else:
                        h, chunk = divmod(n, NCH)
                        pe.wait_ge(S[f"f_wqk{h}"], 16)
                        qk_project(pe, pv[i % 2][:, :], WQ[h], XH, XL, chunk).then_inc(S["f_qk"], 1)
                elif o[0] == "T":
                    if n >= 2:
                        pe.wait_ge(S["b_copy"], n - 1)
                    for t in range(CT):
                        mm = pe.transpose(pa[n % 2][:, t * P:(t + 1) * P], X1[:, t, n * P:(n + 1) * P], ident[:, :])
                    mm.then_inc(S["b_tok"], 1)
                elif o[0] == "F":
                    if n == 0:
                        pe.wait_ge(S["b_feat"], 1)
                        pe.wait_ge(S["b_copy"], ST)
                    if n >= 2:
                        pe.wait_ge(S["b_ftc"], n - 1)
                    for k in range(4):
                        nib, s = divmod(4 * n + k, ST)
                        mm = pe.transpose(pa[n % 2][0:NF, k * P:(k + 1) * P], F[:, s, nib, :], ident[:, :])
                    mm.then_inc(S["b_ft"], 1)
                elif o[0:2] == "L0":
                    q = int(o[2])
                    pe.wait_ge(S["b_ftc"], q + 1)
                    for m in range(3):
                        if q >= 1:
                            pe.wait_ge(S["b_h1lo"], 3 * (q - 1) + m + 1)
                        pe.matmul(ph[m][:, :], W0[:, m, :], FT[:, q * 512:(q + 1) * 512], start=True, stop=True)\
                          .then_inc(S["b_l0"], 1)
                elif o[0:2] == "L1":
                    q = int(o[2])
                    if q == 0:
                        pe.wait_ge(S["b_ftc"], NQ)
                    for m in range(2):
                        if q >= 1:
                            pe.wait_ge(S["b_h2lo"], 2 * (q - 1) + m + 1)
                        i = 0
                        for k in range(3):
                            if m == 0:
                                pe.wait_ge(S["b_h1lo"], 3 * q + k + 1)
                            K = P if k < 2 else 2 * TAIL + 2
                            for w, hh in ((W1H, H1H), (W1L, H1H), (W1H, H1L)):
                                mm = pe.matmul(pa[m][:, :], w[0:K, k, m * P:(m + 1) * P], hh[q % 2][0:K, k, :],
                                               start=(i == 0), stop=(i == 8))
                                i += 1
                        mm.then_inc(S["b_l1"], 1)
                elif o[0:2] == "L2":
                    q = int(o[2])
                    pe.wait_ge(S["b_h2lo"], 2 * (q + 1))
                    if q >= 1:
                        pe.wait_ge(S["b_yf"], q)
                    for m in range(2):
                        K = P if m == 0 else TAIL + 2
                        pe.matmul(py[:, :], W2S[0:K, m, :], H2H[0:K, m, :], start=(m == 0), stop=False)
                        mm = pe.matmul(py[:, :], W2S[0:K, m, :], H2L[0:K, m, :], start=False, stop=(m == 1))
                    mm.then_inc(S["b_l2"], 1)
                elif o[0] == "Y":
                    pe.wait_ge(S["b_yf"], NQ)
                    for j in range(2 * ST):
                        mm = pe.transpose(pa[0][:, 8 * j:8 * j + 8], YF[:, j * P:(j + 1) * P], ident[0:8, 0:8])
                    mm.then_inc(S["b_yt"], 1)
                elif o[0] == "R":
                    if n == 0:
                        pe.wait_ge(S["b_add"], 1)
                    if n >= 2:
                        pe.wait_ge(S["b_out"], n - 1)
                    for t in range(CT):
                        mm = pe.transpose(pa[n % 2][:, t * P:(t + 1) * P], X1[:, t, n * P:(n + 1) * P], ident[:, :])
                    mm.then_inc(S["b_back"], 1)

        @block.scalar
        def _(act):
            for o in order:
                n = int(o[1:])
                i = projected.index(o) if o in projected else 0
                if o[0] == "V":
                    act.wait_ge(S["f_v"], n + 1)
                    act.activation(VS[:, n, :, 0:D], pv[i % 2][:, :].rearrange("p (h d) -> p h d", h=HEADS),
                                   ACT.Copy).then_inc(S["f_vhi"], 1)
                elif o[0] == "Q":
                    h, chunk = divmod(n, NCH)
                    cs = slice(chunk * 512, (chunk + 1) * 512)
                    if n == 0 and not back:
                        act.wait_ge(S["wv_out"], 32)
                    act.wait_ge(S["f_qk"], n + 1)
                    act.activation(QS[h][0:D, cs], pv[i % 2][0:D, :], ACT.Identity, bias=b_qk[0:D, h:h + 1])
                    act.activation(KH[h][D:P, cs], pv[i % 2][D:P, :], ACT.Identity, bias=b_qk[D:P, h:h + 1])\
                       .then_inc(S["f_qk_hi"], 1)
                elif o[0] == "T":
                    act.wait_ge(S["b_tok"], n + 1)
                    act.activation(tile(n), pa[n % 2][:, :].rearrange("p (t n) -> p t n", t=CT), ACT.Copy)\
                       .then_inc(S["b_copy"], 1)
                elif o == "S0":
                    act.wait_ge(S["b_var"], 1)
                    act.activation(std[:, :], ev[:, :], ACT.Sqrt).then_inc(S["b_std"], 1)
                elif o[0] == "F":
                    act.wait_ge(S["b_ft"], n + 1)
                    act.activation(FT[:, n * 512:(n + 1) * 512], pa[n % 2][0:NF, :], ACT.Copy)\
                       .then_inc(S["b_ftc"], 1)
                elif o[0:2] == "L0":
                    q = int(o[2])
                    for m in range(3):
                        act.wait_ge(S["b_l0"], 3 * q + m + 1)
                        if q >= 2 and m == 0:
                            act.wait_ge(S["b_l1"], 2 * (q - 1))
                        act.activation(H1H[q % 2][:, m, :], ph[m][:, :], ACT.Relu).then_inc(S["b_h1hi"], 1)
                elif o[0:2] == "L1":
                    q = int(o[2])
                    for m in range(2):
                        act.wait_ge(S["b_l1"], 2 * q + m + 1)
                        if q >= 1 and m == 0:
                            act.wait_ge(S["b_l2"], q)
                        act.activation(H2H[:, m, :], pa[m][:, :], ACT.Relu).then_inc(S["b_h2hi"], 1)
                elif o[0:2] == "L2":
                    q = int(o[2])
                    act.wait_ge(S["b_l2"], q + 1)
                    act.activation(YF[:, q * 512:(q + 1) * 512], py[0:8, :], ACT.Copy).then_inc(S["b_yf"], 1)
                elif o[0] == "R":
                    act.wait_ge(S["b_back"], n + 1)
                    act.activation(tile(n), pa[n % 2][:, :].rearrange("p (t n) -> p t n", t=CT), ACT.Copy)\
                       .then_inc(S["b_out"], 1)

        @block.vector
        def _(dve):
            if not back:
                dve.memset(T["OT"][:, 0, 0:1], 0.0).then_inc(S["b_store"], 16 * NCH)
            count = [0]

            def step(ins):
                ins.then_inc(S["b_vec"], 1)
                count[0] += 1
                dve.wait_ge(S["b_vec"], count[0])

            def rstd():
                dve.wait_ge(S["b_stat"], ST)
                for s in range(ST):
                    dve.bn_aggr(mv[:, s, :], stats[:, s, :]).then_inc(S["b_stat"], 1)
                dve.wait_ge(S["b_stat"], 2 * ST)
                dve.tensor_scalar(ev[:, :], mv[:, :, 1], 1e-5, None, ALU.add).then_inc(S["b_var"], 1)
                dve.memset(F[:, :, :, :], 0.0)
                dve.memset(G[:, :, :, :], 1.0)
                rstd_of(dve, S["b_var"], S["b_std"], std[:, :], r[:, :], tmp[:, :], nb[:, :],
                        mv[:, :, 0], ev[:, :], 1)
                step(dve.tensor_scalar(r1[:, :], r[:, :], 1.0, None, ALU.add))

            def select():
                for s in range(ST):
                    last = dve.tensor_scalar(XN[:, s, :], X1[:, 0, s * P:s * P + SEL], r[:, s:s + 1], nb[:, s:s + 1],
                                             ALU.mult, ALU.add)
                last.then_inc(S["b_sel"], 1)
                dve.wait_ge(S["b_sel"], 1)

            def nibbles():
                group = above[:, :, :].rearrange("p s (g k) -> p (s g) k", k=16)
                step(dve.tensor_scalar(above[:, :, :], XN[:, :, 16:80], 0.5, None, ALU.is_gt))
                step(dve.tensor_tensor(group, group, T["ramp"][:, :].unsqueeze(1).to_broadcast([P, ST * 4, 16]),
                                       ALU.mult))
                flat = idx[:, :, :, :].rearrange("p s a b -> p (s a b)")
                step(dve.tensor_reduce(flat, group, AX.X, ALU.max))
                step(dve.tensor_scalar(tmp16[:, :], flat, -1.0, 16.0, ALU.mult, ALU.add))
                step(dve.scalar_tensor_tensor(out=flat, in0=flat, scalar=0.5, in1=tmp16[:, :],
                                              op0=ALU.is_gt, op1=ALU.mult))

            def features():
                step(dve.tensor_scalar(cmp3[:, :, :], XN[:, :, 0:3], 0.5, None, ALU.is_gt))
                dve.tensor_tensor(mask[:, :, 0], cmp3[:, :, 0], cmp3[:, :, 1], ALU.mult)
                dve.tensor_tensor(mtmp[:, :, 0], cmp3[:, :, 0], cmp3[:, :, 2], ALU.mult)
                dve.tensor_copy(XNR[:, :, :], XN[:, :, 105:107])
                step(dve.tensor_scalar(mtmp[:, :, 1], cmp3[:, :, 1], -1.0, 1.0, ALU.mult, ALU.add))
                step(dve.tensor_tensor(mask[:, :, 1], mtmp[:, :, 0], mtmp[:, :, 1], ALU.mult))
                dve.tensor_tensor(active[:, :], mask[:, :, 0], mask[:, :, 1], ALU.add)
                dve.tensor_tensor(XNL[:, :, :], XN[:, :, 105:107], f32(XNR[:, :, :]), ALU.subtract)
                for nib in range(2):
                    dve.tensor_copy(G[:, :, nib, 0:2], idx[:, :, :, nib])
                    last = dve.tensor_copy(G[:, :, nib, 2:4], f32(XNR[:, :, :]))
                step(last)
                for net in range(2):
                    mk = mask[:, :, net:net + 1]
                    for nib in range(2):
                        for base in (5 * net, 10 + 5 * net):
                            dve.tensor_tensor(F[:, :, nib, base:base + 5], G[:, :, nib, :],
                                              mk.to_broadcast([P, ST, 5]), ALU.mult)
                        for base in (20 + 2 * net, 24 + 2 * net):
                            last = dve.tensor_tensor(F[:, :, nib, base:base + 2], XNL[:, :, :],
                                                     mk.to_broadcast([P, ST, 2]), ALU.mult)
                last.then_inc(S["b_feat"], 1)

            def results():
                dve.wait_ge(S["b_yt"], 1)
                step(dve.tensor_copy(Y8[:, :, :].rearrange("p j k -> p (j k)"), pa[0][:, 0:16 * ST]))
                step(dve.tensor_tensor(Y4[:, :, :], Y8[:, :, 0:4], Y8[:, :, 4:8], ALU.add))
                for nib in range(2):
                    for v in range(2):
                        y = Y4[:, nib * ST:(nib + 1) * ST, 2 * v:2 * v + 2]
                        last = dve.tensor_tensor(y, y, mask[:, :, :], ALU.mult)
                step(last)
                for nib in range(2):
                    y = Y4[:, nib * ST:(nib + 1) * ST, :].rearrange("p s (v e) -> p s v e", e=2)
                    last = dve.tensor_tensor(YS[:, :, nib, :], y[:, :, :, 0], y[:, :, :, 1], ALU.add)
                step(last)
                step(dve.tensor_scalar(YR[:, :, :], YS[:, :, :, 0], -1.0, 16.0, ALU.max, ALU.min))
                step(dve.tensor_scalar(YR[:, :, :], YR[:, :, :], ROUND, None, ALU.add))
                step(dve.tensor_scalar(YR[:, :, :], YR[:, :, :], ROUND, None, ALU.subtract))
                step(dve.tensor_scalar(YR[:, :, :], YR[:, :, :], 0.0, 15.0, ALU.max, ALU.min))
                step(dve.scalar_tensor_tensor(out=YR[:, :, :], in0=YR[:, :, :], scalar=1.0,
                                              in1=active[:, :].unsqueeze(2).to_broadcast([P, ST, 2]),
                                              op0=ALU.add, op1=ALU.mult))
                step(dve.tensor_scalar(YR[:, :, :], YR[:, :, :], -1.0, None, ALU.add))
                dve.tensor_scalar(CY[:, :], YS[:, :, 1, 1], 0.5, None, ALU.is_gt)
                for nib in range(2):
                    last = dve.tensor_tensor(EQ[:, :, nib, :], T["iota"][:, :].unsqueeze(1).to_broadcast([P, ST, 16]),
                                             YR[:, :, nib:nib + 1].to_broadcast([P, ST, 16]), ALU.is_equal)
                step(last)
                dve.wait_ge(S["b_scale"], ST)
                wide = X1[:, 1, :].rearrange("p (s n) -> p s n", n=P)
                dve.scalar_tensor_tensor(out=wide[:, :, 0:32], in0=EQ[:, :, :, :].rearrange("p s n k -> p s (n k)"),
                                         scalar=2.0, in1=wide[:, :, 0:32], op0=ALU.mult, op1=ALU.add)
                dve.tensor_tensor(wide[:, :, 32], wide[:, :, 32], CY[:, :], ALU.add).then_inc(S["b_add"], 1)

            for o in order:
                n = int(o[1:])
                i = projected.index(o) if o in projected else 0
                if o[0] == "V":
                    dve.wait_ge(S["f_vhi"], n + 1)
                    dve.tensor_tensor(VS[:, n, :, D:2 * D], pv[i % 2][:, :].rearrange("p (h d) -> p h d", h=HEADS),
                                      f32(VS[:, n, :, 0:D]), ALU.subtract).then_inc(S["f_vlo"], 1)
                elif o[0] == "Q":
                    h, chunk = divmod(n, NCH)
                    dve.wait_ge(S["f_qk_hi"], n + 1)
                    split_qk(dve, pv[i % 2], QS[h], KH[h], KL[h], b_qk[:, h:h + 1], chunk)\
                        .then_inc(S["f_qk_lo"], 1)
                elif o[0] == "T":
                    dve.wait_ge(S["b_copy"], n + 1)
                    dve.bn_stats(stats[:, n, :], tile(n)).then_inc(S["b_stat"], 1)
                elif o == "S0":
                    rstd()
                elif o == "S1":
                    select()
                elif o == "S2":
                    nibbles()
                elif o == "S3":
                    features()
                elif o == "S4":
                    results()
                elif o[0:2] == "L0":
                    q = int(o[2])
                    for m in range(3):
                        dve.wait_ge(S["b_h1hi"], 3 * q + m + 1)
                        dve.scalar_tensor_tensor(out=H1L[q % 2][:, m, :], in0=ph[m][:, :], scalar=0.0,
                                                 in1=f32(H1H[q % 2][:, m, :]), op0=ALU.max, op1=ALU.subtract)\
                           .then_inc(S["b_h1lo"], 1)
                elif o[0:2] == "L1":
                    q = int(o[2])
                    for m in range(2):
                        dve.wait_ge(S["b_h2hi"], 2 * q + m + 1)
                        dve.scalar_tensor_tensor(out=H2L[:, m, :], in0=pa[m][:, :], scalar=0.0,
                                                 in1=f32(H2H[:, m, :]), op0=ALU.max, op1=ALU.subtract)\
                           .then_inc(S["b_h2lo"], 1)


def split_qk(dve, bank, QSb, KHb, KLb, bias, n):
    cs = slice(n * 512, (n + 1) * 512)
    dve.scalar_tensor_tensor(out=QSb[D:P, cs], in0=bank[0:D, :], scalar=bias[0:D, :], in1=f32(QSb[0:D, cs]),
                             op0=ALU.add, op1=ALU.subtract)
    return dve.scalar_tensor_tensor(out=KLb[D:P, cs], in0=bank[D:P, :], scalar=bias[D:P, :],
                                    in1=f32(KHb[D:P, cs]), op0=ALU.add, op1=ALU.subtract)


def attention(nc, tag, S, dram, T, nxt):
    with ExitStack() as c:
        def sb(name, shape, dt=F32):
            return c.enter_context(nc.sbuf_tensor(f"{name}_{tag}", shape, dt))

        XH, XL, VS, QS, WQ = (T[k] for k in ("XH", "XL", "VS", "QS", "WQ"))
        KH, KL = ([z[:, i, :] for z in T["KHL"]] for i in range(2))
        ident, b_qk, b_v, OT = (T[k] for k in ("ident", "b_qk", "b_v", "OT"))

        PH = [sb(f"PH{i}", [P, ST, 512], F32R) for i in (1, 0)][::-1]
        PL = [sb(f"PL{i}", [P, ST, 512], F32R) for i in range(2)]
        PR = [sb(f"PR{i}", [P, HW]) for i in range(2)]
        OB = [sb(f"OB{i}", [D, 512]) for i in range(2)]
        QK = sb("QK", [P, 512])
        HL = sb("HL", [P, 2, 512], F32R)
        nmax = sb("nmax", [P, STEPS])
        rsum = sb("rsum", [P, STEPS])
        rinv = sb("rinv", [P, STEPS])
        pS = [c.enter_context(nc.psum_tensor(f"pS{i}_{tag}", [P, HW], F32)) for i in range(2)]
        pT = [c.enter_context(nc.psum_tensor(f"pT{i}_{tag}", [P, 512], F32)) for i in range(2)]
        pJ = c.enter_context(nc.psum_tensor(f"pJ_{tag}", [P, 512], F32))
        pO = c.enter_context(nc.psum_tensor(f"pO_{tag}", [P, 512], F32))
        block = c.enter_context(nc.Block())

        def projection(g):
            head, r = (g + 6) // ST + 1, (g + 6) % ST
            if head <= 2:
                return (2, 1, 4 * (g - 1), 4 * g) if 1 <= g <= 3 else None
            return (head, r // 4) + ((0, 2), (2, 5), (5, 10), (10, 12))[r % 4] if head < HEADS else None

        def copying(g):
            head, r = (g + 2) // ST + 1, (g + 2) % ST
            if head <= 2:
                return (2, g // 4) if g in (0, 4) else None
            return (head, r // 4) if r % 4 == 0 and head < HEADS else None

        def splitting(g):
            return {0: (2, 0), 8: (2, 1)}.get(g) if g < 14 else copying(g)

        @block.sync
        def _(sp):
            def weights(h):
                sp.dma_start(f32(WQ[h % 2][:, :, :, :].rearrange("p a k n -> p a (k n)")), dram["wqk"][h])\
                  .then_inc(S[f"a_w{h % 2}"], 16)

            for h in range(2, HEADS):
                sp.wait_ge(S["a_scores"], ST * (h - 1))
                for n in range(NCH):
                    cs = slice(n * 512, (n + 1) * 512)
                    sp.wait_ge(S["a_proj_lo"], NCH * (h - 2) + n + 1)
                    for half in range(2):
                        ps = slice(half * D, (half + 1) * D)
                        sp.dma_start(f32(QS[h % 2][ps, cs]), f32(HL[0:D, half, :])).then_inc(S["a_qk"], 16)
                        sp.dma_start(f32(T["KHL"][h % 2][ps, :, cs]), f32(HL[D:P, :, :])).then_inc(S["a_qk"], 16)
                if h + 2 < HEADS:
                    weights(h + 2)
            sp.wait_ge(S["a_proj"], NCH * (HEADS - 2))
            for k in range(2):
                sp.dma_start(f32(T["WO"][:, k, :, :].rearrange("p k n -> p (k n)")), dram["wo"][:, k, :])\
                  .then_inc(S["b_wo"], 16)
            if nxt is not None:
                for t in range(CT):
                    sp.dma_start(T["X"][:, t, :], dram["x"][nxt, :, t, :]).then_inc(S["f_x"], 16)
            sp.wait_ge(S["a_qk"], 64 * NCH * (HEADS - 2))

        @block.tensor
        def _(pe):
            def scores(g):
                h, t = divmod(g, ST)
                if t == 0 and h < 2:
                    pe.wait_ge(S[f"f_kdup{h}"], 16)
                if t == 0 and h >= 2:
                    pe.wait_ge(S["a_qk"], 64 * NCH * (h - 1))
                if g >= 2:
                    pe.wait_ge(S["a_exp"], g - 1)
                q = QS[h % 2][:, t * P:(t + 1) * P]
                for n in range(NCH):
                    cs = slice(n * 512, (n + 1) * 512)
                    pe.matmul(pS[g % 2][:, cs], q, KH[h % 2][:, cs], start=True, stop=False)
                    mm = pe.matmul(pS[g % 2][:, cs], q, KL[h % 2][:, cs], start=False, stop=True)
                mm.then_inc(S["a_scores"], 1)

            def turn(g):
                pe.wait_ge(S["a_norm"], g + 1)
                for half in range(2):
                    if g >= 1:
                        pe.wait_ge(S["a_lo"], 2 * (g - 1) + half + 1)
                    for k in range(4):
                        kb = 4 * half + k
                        mm = pe.transpose(pT[half][:, k * P:(k + 1) * P], PR[g % 2][:, kb * P:(kb + 1) * P],
                                          ident[:, :])
                    mm.then_inc(S["a_tr"], 1)

            def project(h, chunk, *part):
                if part[0] == 0:
                    pe.wait_ge(S[f"a_w{h % 2}"], 16 * (h // 2))
                    if 2 * (h - 2) + chunk > 0:
                        pe.wait_ge(S["a_proj_out"], 2 * (h - 2) + chunk)
                mm = qk_project(pe, pJ[:, :], WQ[h % 2], XH, XL, chunk, part)
                if part[1] == 12:
                    mm.then_inc(S["a_proj"], 1)

            def values(ck, part):
                h = ck // 2
                if part[0] == 0:
                    pe.wait_ge(S["a_lo"], 8 * (ck + 1))
                    if ck >= 1:
                        pe.wait_ge(S["a_o"], ck)
                for kb in range(*part):
                    v = VS[:, kb, h, :]
                    pe.matmul(pO[:, :], v, PH[ck % 2][:, kb, :], start=(kb == 0), stop=False)
                    mm = pe.matmul(pO[:, :], v, PL[ck % 2][:, kb, :], start=False, stop=(kb == ST - 1))
                if part[1] == ST:
                    mm.then_inc(S["a_pv"], 1)

            scores(0)
            scores(1)
            project(2, 0, 0, 12)
            for g in range(STEPS + 4):
                if g + 2 < STEPS:
                    scores(g + 2)
                if g >= 4 and g % 4 > 0:
                    values(g // 4 - 1, ((0, 3), (3, 6), (6, 8))[g % 4 - 1])
                if g < STEPS:
                    turn(g)
                if projection(g):
                    project(*projection(g))

        @block.scalar
        def _(act):
            def exp(g):
                act.wait_ge(S["a_max"], g + 1)
                if g >= 2:
                    act.wait_ge(S["a_tr"], 2 * (g - 1))
                act.activation(PR[g % 2][:, :], pS[g % 2][:, :], ACT.Exp, bias=nmax[:, g:g + 1],
                               accum_out=rsum[:, g:g + 1]).then_inc(S["a_exp"], 1)

            exp(0)
            for g in range(STEPS + 5):
                if g + 1 < STEPS:
                    exp(g + 1)
                if g >= 8 and g % 4 == 0:
                    ck = g // 4 - 2
                    act.wait_ge(S["a_pv"], ck + 1)
                    if ck >= 2:
                        act.wait_ge(S["a_o"], ck - 1)
                    act.activation(OB[ck % 2][:, :], pO[D:P, :], ACT.Identity,
                                   bias=b_v[D:P, ck // 2:ck // 2 + 1]).then_inc(S["a_obot"], 1)
                if copying(g):
                    h, n = copying(g)
                    i = NCH * (h - 2) + n
                    act.wait_ge(S["a_proj"], i + 1)
                    if i > 0:
                        act.wait_ge(S["a_proj_lo"], i)
                    act.activation(QK[:, :], pJ[:, :], ACT.Identity, bias=b_qk[:, h:h + 1])\
                       .then_inc(S["a_proj_out"], 1)
                if g < STEPS:
                    ck = g // 4
                    if ck >= 2:
                        act.wait_ge(S["a_pv"], ck - 1)
                    elif g == 4:
                        act.wait_ge(S["b_store"], 16 * NCH)
                    for half in range(2):
                        act.wait_ge(S["a_tr"], 2 * g + half + 1)
                        act.activation(PH[ck % 2][:, 4 * half:4 * half + 4, (g % 4) * P:(g % 4 + 1) * P],
                                       pT[half][:, :].rearrange("p (k n) -> p k n", k=4), ACT.Copy)\
                           .then_inc(S["a_hi"], 1)
                if splitting(g):
                    h, n = splitting(g)
                    i = NCH * (h - 2) + n
                    act.wait_ge(S["a_proj_out"], i + 1)
                    if i > 0:
                        act.wait_ge(S["a_qk"], 64 * i)
                    act.activation(HL[:, 0, :], QK[:, :], ACT.Copy).then_inc(S["a_proj_hi"], 1)

        @block.vector
        def _(dve):
            def rowmax(g):
                dve.wait_ge(S["a_scores"], g + 1)
                dve.tensor_reduce(nmax[:, g:g + 1], pS[g % 2][:, :], AX.X, ALU.max, negate=True)\
                   .then_inc(S["a_max"], 1)

            def recip(g):
                dve.wait_ge(S["a_exp"], g + 1)
                dve.reciprocal(rinv[:, g:g + 1], rsum[:, g:g + 1]).then_inc(S["a_recip"], 1)

            rowmax(0)
            rowmax(1)
            recip(0)
            for g in range(STEPS + 5):
                if g + 2 < STEPS:
                    rowmax(g + 2)
                if g + 1 < STEPS:
                    recip(g + 1)
                if g >= 8 and g % 4 == 0:
                    ck = g // 4 - 2
                    hh, n = divmod(ck, 2)
                    dve.wait_ge(S["a_obot"], ck + 1)
                    by_query = [z.rearrange("d (m jj jp) -> d jp jj m", jp=2, jj=CT) for z in (pO[0:D, :], OB[ck % 2][:, :])]
                    cols = slice(hh * P + n * D, hh * P + (n + 1) * D)
                    for jp in range(2):
                        last = dve.tensor_tensor(OT[jp * D:(jp + 1) * D, :, cols], by_query[0][:, jp], by_query[1][:, jp],
                                                 ALU.add)
                    last.then_inc(S["a_o"], 1)
                if g < STEPS:
                    ck = g // 4
                    for half in range(2):
                        ks = slice(4 * half, 4 * half + 4)
                        qs = slice((g % 4) * P, (g % 4 + 1) * P)
                        dve.wait_ge(S["a_hi"], 2 * g + half + 1)
                        dve.tensor_tensor(PL[ck % 2][:, ks, qs], pT[half][:, :].rearrange("p (k n) -> p k n", k=4),
                                          f32(PH[ck % 2][:, ks, qs]), ALU.subtract).then_inc(S["a_lo"], 1)

        @block.gpsimd
        def _(pool):
            for g in range(STEPS):
                pool.wait_ge(S["a_recip"], g + 1)
                pool.tensor_scalar(PR[g % 2][:, :], PR[g % 2][:, :], rinv[:, g:g + 1], 1.0, ALU.mult, ALU.mult)\
                    .then_inc(S["a_norm"], 1)
                if g >= 1 and splitting(g - 1):
                    h, n = splitting(g - 1)
                    i = NCH * (h - 2) + n
                    pool.wait_ge(S["a_proj_hi"], i + 1)
                    pool.tensor_tensor(HL[:, 1, :], QK[:, :], f32(HL[:, 0, :]), ALU.subtract)\
                        .then_inc(S["a_proj_lo"], 1)


def kernel(x, L0_conv_Wq, L0_conv_bq, L0_conv_Wk, L0_conv_bk, L0_conv_Wv, L0_conv_bv, L0_conv_Wo, L0_conv_bo,
           L0_ffn_Wa, L0_ffn_ba, L0_ffn_Ws, L0_ffn_bs):
    import numpy as np
    import concourse.bacc as bacc
    from concourse.bass_utils import run_bass_kernel_spmd

    f = np.float32
    x, wq, bq, wk, bk, wv, bv, wo, bo, wa, ba, ws, bs = [
        np.asarray(a) for a in (x, L0_conv_Wq, L0_conv_bq, L0_conv_Wk, L0_conv_bk, L0_conv_Wv, L0_conv_bv,
                                L0_conv_Wo, L0_conv_bo, L0_ffn_Wa, L0_ffn_ba, L0_ffn_Ws, L0_ffn_bs)]

    def by_channel(w):
        return w.T.reshape(CT, P, -1).transpose(1, 0, 2)

    q4, k4 = (by_channel(w).reshape(P, CT, HEADS, D).transpose(0, 2, 1, 3) for w in (wq, wk))
    wqk = np.concatenate([q4, k4], axis=3).reshape(P, -1)
    bqk = np.concatenate([bq.reshape(HEADS, D).T, bk.reshape(HEADS, D).T], axis=0)

    w0 = np.zeros((NF, 3, P), f)
    for net, (w, b) in enumerate(((wa, ba), (ws, bs))):
        cols = [w[0][:, i] for i in (0, 1, 35, 36)] + [b[0]]
        rows = [(5 * net + i, i) for i in range(5)] + [(10 + 5 * net + i, i) for i in range(5)]
        rows += [(20 + 2 * net + i, 2 + i) for i in range(2)] + [(24 + 2 * net + i, 2 + i) for i in range(2)]
        for row, i in rows:
            w0[row, net, :] = cols[i][0:P]
            w0[row, 2, net * TAIL:(net + 1) * TAIL] = cols[i][P:GE]
            if i == 4:
                w0[row, 2, 2 * TAIL + net] = 1.0
    takes_hi = np.array([1] * 10 + [0] * 10 + [1] * 4 + [0] * 8, f)
    w0mask = np.stack([takes_hi, 1 - takes_hi], axis=1)
    w1 = np.zeros((P, 3, 2, P), f)
    w2 = np.zeros((P, 2, P - 4), f)
    for net, (w, b) in enumerate(((wa, ba), (ws, bs))):
        wt = w[1].T
        for m, (o0, o1) in enumerate(((0, P), (P, GE))):
            w1[:, net, m, 0:o1 - o0] = wt[0:P, o0:o1]
            w1[net * TAIL:(net + 1) * TAIL, 2, m, 0:o1 - o0] = wt[P:GE, o0:o1]
            w1[2 * TAIL + net, 2, m, 0:o1 - o0] = b[1][o0:o1]
        w1[2 * TAIL + net, 2, 1, TAIL + net] = 1.0
        for v, o in enumerate((100, 101)):
            w2[:, 0, 2 * v + net] = w[2][o, 0:P]
            w2[0:TAIL, 1, 2 * v + net] = w[2][o, P:GE]
            w2[TAIL + net, 1, 2 * v + net] = b[2][o]

    arrays = {
        "x": x.reshape(N_IMG, C, HW),
        "wqk": wqk,
        "bqk": bqk,
        "wv": by_channel(wv).reshape(P, -1),
        "wo": by_channel(wo).reshape(P, -1),
        "bv": bv.reshape(HEADS, D).T,
        "bo_rep": np.repeat(bo[None, :], P, axis=0),
        "w0": w0.reshape(NF, -1),
        "w0mask": w0mask,
        "w1": w1.reshape(P, -1),
        "w2": w2,
        "ident": np.eye(P, dtype=f),
        "ramp": np.tile(np.arange(16, 0, -1, dtype=f)[None, :], (P, 1)),
        "iota": np.tile(np.arange(16, dtype=f)[None, :], (P, 1)),
    }
    arrays = {"in_" + k: np.ascontiguousarray(v) for k, v in arrays.items()}
    nc = bacc.Bacc("TRN2", target_bir_lowering=False, num_devices=1)
    aps = [nc.dram_tensor(k, v.shape, mybir.dt.from_np(v.dtype), kind="ExternalInput").ap()
           for k, v in arrays.items()]
    out = nc.dram_tensor("out_0", (N_IMG, C, HW), F32, kind="ExternalOutput").ap()
    build(nc, *aps, out)
    r = run_bass_kernel_spmd(nc, [arrays], core_ids=[0])
    return r.results[0]["out_0"].reshape(N_IMG, C, 32, 32)
```
